# Optimizing a Trainium2 kernel written in Bass

```python
import numpy as np
import jax
import jax.numpy as jnp

def _softmax(x, axis=-1):
    return jax.nn.softmax(x, axis=axis)

def _gelu(x):
    return jax.nn.gelu(x, approximate=True)

def _silu(x):
    return jax.nn.silu(x)

def _sigmoid(x):
    return jax.nn.sigmoid(x)

def _layernorm(x, axis=-1, eps=1e-05):
    m = jnp.mean(x, axis=axis, keepdims=True)
    v = jnp.var(x, axis=axis, keepdims=True)
    return (x - m) / jnp.sqrt(v + eps)

def _scatter_add(tgt, idx, src, axis=0):
    return tgt.at[idx].add(src)

def _segment_sum(src, seg, n):
    return jax.ops.segment_sum(src, seg, n)
kernel_name = 'mk_flamingo_gated_d1_seqx_r8_808dc8'

def setup_inputs(seed: int=0):
    np.random.seed(seed)
    _w = jnp.asarray

    def _rec_inputs():
        import jax
        import jax.numpy as jnp
        _rk = jax.random.key(seed)
        x = 7.22e-05 + 1 * jax.random.normal(jax.random.fold_in(_rk, 1), (2, 512, 128), jnp.float32)
        _lenS = 512 - jax.random.randint(jax.random.fold_in(_rk, 7), (2,), 0, max(1, 512 // 4) + 1, jnp.int32)
        _lenS2 = 32 - jax.random.randint(jax.random.fold_in(_rk, 8), (2,), 0, max(1, 32 // 4) + 1, jnp.int32)
        _ctx_1024P = jax.random.normal(jax.random.fold_in(_rk, 11), (2, 16, 128), jnp.float32)
        _ctx_1024c = jax.random.dirichlet(jax.random.fold_in(_rk, 511), 0.3 * jnp.ones((16,), jnp.float32), (2, 32))
        _ctx_1024t = jnp.einsum('bsk,bkd->bsd', _ctx_1024c, _ctx_1024P)
        _ctx_1024t = _ctx_1024t * jax.lax.rsqrt(jnp.mean(jnp.square(_ctx_1024t)) + 1e-12) * 0.953939
        ctx_1024 = 4.13588e-05 + 0.999923 * (_ctx_1024t + 0.3 * jax.random.normal(jax.random.fold_in(_rk, 611), (2, 32, 128), jnp.float32))
        _g = jax.random.normal(jax.random.fold_in(_rk, 9001), (2, 1), jnp.float32)
        _g = jnp.sign(_g) * jnp.maximum(jnp.abs(_g), 1.0) + (_g == 0) * 1.0
        g_xattn = _g[0]
        g_ffn = _g[1]
        return (x, ctx_1024, g_xattn, g_ffn)
    x, ctx_1024, g_xattn, g_ffn = _rec_inputs()

    def _L0_xattn_setup():
        import jax, jax.numpy as jnp
        import numpy as np
        EMBED = 128
        HEADS = 16
        HEAD_DIM = EMBED // HEADS
        key = jax.random.key(seed)
        ks = jax.random.split(key, 10)
        B, N, M = (4, 256, 256)
        s = 1.0 / np.sqrt(EMBED)
        return {'xq': jax.random.normal(ks[0], (B, N, EMBED), jnp.float32), 'xk': jax.random.normal(ks[1], (B, M, EMBED), jnp.float32), 'xv': jax.random.normal(ks[2], (B, M, EMBED), jnp.float32), 'Wq': jax.random.normal(ks[3], (EMBED, EMBED), jnp.float32) * s, 'bq': jnp.zeros((EMBED,), jnp.float32), 'Wk': jax.random.normal(ks[4], (EMBED, EMBED), jnp.float32) * s, 'bk': jnp.zeros((EMBED,), jnp.float32), 'Wv': jax.random.normal(ks[5], (EMBED, EMBED), jnp.float32) * s, 'bv': jnp.zeros((EMBED,), jnp.float32), 'Wo': jax.random.normal(ks[6], (EMBED, EMBED), jnp.float32) * s}
    _L0_xattn_all = _L0_xattn_setup()
    _L0_xattn_in = {k: v for k, v in _L0_xattn_all.items() if k in ('Wq', 'bq', 'Wk', 'bk', 'Wv', 'bv', 'Wo')}
    del _L0_xattn_all

    def _L0_ffn_setup():
        import jax, jax.numpy as jnp
        import numpy as np
        HIDDEN = 128
        INTER = 512
        N_EXPERTS = 8
        TOP_K = 2
        INIT_STD = 0.02
        key = jax.random.key(seed)
        ks = jax.random.split(key, 6)
        x = jax.random.normal(ks[0], (2, 128, HIDDEN), dtype=jnp.float32)
        Wg = jax.random.normal(ks[1], (N_EXPERTS, HIDDEN), dtype=jnp.float32) * INIT_STD
        W1 = jax.random.normal(ks[2], (N_EXPERTS, HIDDEN, INTER), dtype=jnp.float32) * INIT_STD
        b1 = jnp.zeros((N_EXPERTS, INTER), dtype=jnp.float32)
        W2 = jax.random.normal(ks[3], (N_EXPERTS, INTER, HIDDEN), dtype=jnp.float32) * INIT_STD
        b2 = jnp.zeros((N_EXPERTS, HIDDEN), dtype=jnp.float32)
        return {'x': x, 'Wg': Wg, 'W1': W1, 'b1': b1, 'W2': W2, 'b2': b2}
    _L0_ffn_all = _L0_ffn_setup()
    _L0_ffn_in = {k: v for k, v in _L0_ffn_all.items() if k in ('Wg', 'W1', 'b1', 'W2', 'b2')}
    del _L0_ffn_all
    return {'x': x, 'ctx_1024': ctx_1024, 'g_xattn': g_xattn, 'g_ffn': g_ffn, 'L0_xattn_Wq': _L0_xattn_in['Wq'], 'L0_xattn_bq': _L0_xattn_in['bq'], 'L0_xattn_Wk': _L0_xattn_in['Wk'], 'L0_xattn_bk': _L0_xattn_in['bk'], 'L0_xattn_Wv': _L0_xattn_in['Wv'], 'L0_xattn_bv': _L0_xattn_in['bv'], 'L0_xattn_Wo': _L0_xattn_in['Wo'], 'L0_ffn_Wg': _L0_ffn_in['Wg'], 'L0_ffn_W1': _L0_ffn_in['W1'], 'L0_ffn_b1': _L0_ffn_in['b1'], 'L0_ffn_W2': _L0_ffn_in['W2'], 'L0_ffn_b2': _L0_ffn_in['b2']}

def reference(x, ctx_1024, g_xattn, g_ffn, L0_xattn_Wq, L0_xattn_bq, L0_xattn_Wk, L0_xattn_bk, L0_xattn_Wv, L0_xattn_bv, L0_xattn_Wo, L0_ffn_Wg, L0_ffn_W1, L0_ffn_b1, L0_ffn_W2, L0_ffn_b2):
    import jax
    import jax.numpy as jnp

    def _L0_xattn_ref(xq, xk, xv, Wq, bq, Wk, bk, Wv, bv, Wo):
        import jax, jax.numpy as jnp
        import numpy as np
        EMBED = 128
        HEADS = 16
        HEAD_DIM = EMBED // HEADS
        B, N, _ = xq.shape
        M = xk.shape[1]
        scale = HEAD_DIM ** (-0.5)
        q = (xq @ Wq.T + bq).reshape(B, N, HEADS, HEAD_DIM).transpose(0, 2, 1, 3)
        k = (xk @ Wk.T + bk).reshape(B, M, HEADS, HEAD_DIM).transpose(0, 2, 1, 3)
        v = (xv @ Wv.T + bv).reshape(B, M, HEADS, HEAD_DIM).transpose(0, 2, 1, 3)
        scores = jnp.einsum('bhnd,bhmd->bhnm', q, k) * scale
        weights = jax.nn.softmax(scores, axis=-1)
        out = jnp.einsum('bhnm,bhmd->bhnd', weights, v)
        out = out.transpose(0, 2, 1, 3).reshape(B, N, EMBED)
        return out @ Wo.T

    def _L0_ffn_ref(x, Wg, W1, b1, W2, b2):
        import jax, jax.numpy as jnp
        import numpy as np
        HIDDEN = 128
        INTER = 512
        N_EXPERTS = 8
        TOP_K = 2
        INIT_STD = 0.02
        orig_shape = x.shape
        xt = x.reshape(-1, HIDDEN)
        T = xt.shape[0]
        logits = xt @ Wg.T
        topk_logits, topk_idx = jax.lax.top_k(logits, TOP_K)
        w = jax.nn.softmax(topk_logits, axis=-1)
        rows = jnp.arange(T)[:, None]
        gates = jnp.zeros((T, N_EXPERTS), xt.dtype).at[rows, topk_idx].add(w)
        h = jnp.einsum('th,ehi->tei', xt, W1) + b1
        h = jax.nn.gelu(h, approximate=False)
        o = jnp.einsum('tei,eih->teh', h, W2) + b2
        y = jnp.einsum('te,teh->th', gates, o)
        return y.reshape(orig_shape)
    x = x + jnp.tanh(g_xattn[0]) * _L0_xattn_ref(_layernorm(x, axis=-1), ctx_1024, ctx_1024, L0_xattn_Wq, L0_xattn_bq, L0_xattn_Wk, L0_xattn_bk, L0_xattn_Wv, L0_xattn_bv, L0_xattn_Wo)
    x = x + jnp.tanh(g_ffn[0]) * _L0_ffn_ref(_layernorm(x, axis=-1), L0_ffn_Wg, L0_ffn_W1, L0_ffn_b1, L0_ffn_W2, L0_ffn_b2)
    return x

_drawn_inputs = setup_inputs


def setup_inputs(seed=0):
    import zlib

    import numpy as np

    out = dict(_drawn_inputs(seed))
    spreads = {'L0_xattn_bq': (0.0, 0.347),
     'L0_xattn_bk': (0.0, 0.8),
     'L0_xattn_bv': (0.0, 0.1),
     'L0_ffn_b1': (0.0, 0.562),
     'L0_ffn_b2': (0.0, 0.1)}
    factors = {}
    for name, (base, spread) in spreads.items():
        noise = np.random.default_rng([zlib.crc32(name.encode()), seed]).standard_normal(out[name].shape)
        drawn = base * np.exp(spread * noise) if base else spread * noise
        out[name] = jnp.asarray(drawn.astype(out[name].dtype))
    for name, factor in factors.items():
        out[name] = (out[name] * factor).astype(out[name].dtype)
    return out
```

```python
from contextlib import ExitStack

import concourse.bass as bass
from concourse import mybir

ALU = mybir.AluOpType
ACT = mybir.ActivationFunctionType
AX = mybir.AxisListType
F32 = mybir.dt.float32
F16 = mybir.dt.float16
BF16 = mybir.dt.bfloat16

LN_EPS = 1e-5
K_SCALE = 16.0
P_LOG_SCALE = 5.545177444479562
O_SCALE = 16.0
WO_SCALE = 16.0
W_SCALE = 256.0
H_SCALE = 16.0
MASKED = -3.0e38


def gated_block(nc, x, ctx_in, g_xattn, g_ffn, Wq, bq, Wk, bk, Wv, bv, Wo, Wg, W1, b1, W2, b2, out):
    B, N, D = x.shape
    M = ctx_in.shape[1]
    H = 16
    HD = D // H
    E, _, I = W1.shape
    P = 128
    T = N // P
    G = H * M // P
    HG = H // G
    C = I // P
    VC = HG * HD + HG
    BIAS_ROWS = 33
    MAX_ROWS = 32 + H
    GATE_SCALE = 1.0 / (H_SCALE * W_SCALE)
    assert (B, N, D, M, E, I) == (2, 512, 128, 32, 8, 512)
    R_WG, R_B1, R_BQ, R_BK = 0, E, E + E * C, E + E * C + 1
    R_ALL = R_BK + 1
    PAIRS = E // 2

    with ExitStack() as stack:
        def sb(name, shape, dt):
            return stack.enter_context(nc.sbuf_tensor(name, shape, dt))

        def sem(name):
            return stack.enter_context(nc.semaphore(name))

        bank = [stack.enter_context(nc.psum_tensor(f"bank{i}", [P, 512], F32)) for i in range(8)]

        ones = sb("ones", [P, P], F32)
        ident = sb("ident", [P, P], F32)
        ident_b = sb("ident_b", [P, P], BF16)
        ones33 = sb("ones33", [BIAS_ROWS, P], F16)
        head_mask = sb("head_mask", [P, H], F32)
        group_mask = sb("group_mask", [P, G, HG], F32)
        neg_sel = sb("neg_sel", [MAX_ROWS, G, HG, M], BF16)
        expert_no = sb("expert_no", [P, T, E], F32)
        x_sb = sb("x_sb", [P, B, T, D], F32)
        ctx_sb = sb("ctx_sb", [B * M, D], F32)
        wkvo = sb("wkvo", [P, 3, D], F32)
        wq_sb = sb("wq_sb", [P, D], F32)
        smalls = sb("smalls", [R_ALL, D], F32)
        bv_row = sb("bv_row", [1, D], F32)
        g_row = sb("g_row", [1, 2], F32)
        b2_sb = sb("b2_sb", [E, D], F32)
        wT = sb("wT", [P, 3, D], F32)
        ctxT = sb("ctxT", [P, B * M], F32)
        ctxT4 = sb("ctxT4", [P, B, HG, M], F32)
        smallT = sb("smallT", [P, R_ALL], F32)
        bq33 = sb("bq33", [P, BIAS_ROWS], F32)
        tanh_g = sb("tanh_g", [P, 2], F32)
        half_gate = sb("half_gate", [P, 2], F32)
        b2_scaled = sb("b2_scaled", [E, D], F32)
        wo32 = sb("wo32", [P, D], F32)
        wo_hi = sb("wo_hi", [P, D], F16)
        wo_lo = sb("wo_lo", [P, D], F16)
        kT = sb("kT", [P, B, M], F32)
        k_bd = sb("k_bd", [P, B, H, M], F32)
        kq_hi = sb("kq_hi", [P, B, H * M], F16)
        kq_lo = sb("kq_lo", [P, B, H * M], F16)
        bias33 = sb("bias33", [BIAS_ROWS, B, H * M], F16)
        bias_col = sb("bias_col", [P, B, G], F32)
        v32 = sb("v32", [P, B, D], F32)
        vr = sb("vr", [P, B, G, VC], F16)
        v_lo = sb("v_lo", [P, B, G, HG * HD], F16)
        stats = sb("stats", [P, B, T, 6], F32)
        moments = sb("moments", [P, B, T, 2], F32)
        rstd = sb("rstd", [P, B, T], F32)
        neg_half = sb("neg_half", [P, T], F32)
        var_eps = sb("var_eps", [P, B, T], F32)
        xln = sb("xln", [P, B, T, D], F32)
        x_hi = sb("x_hi", [P, B, N], F16)
        x_lo = sb("x_lo", [P, B, N], F16)
        maxes = sb("maxes", [P, B, T, H], F32)
        max_hl = sb("max_hl", [P, B, T, MAX_ROWS], BF16)
        maxT = sb("maxT", [MAX_ROWS, B, N], BF16)
        p32 = sb("p32", [P, 2, N], F32)
        p_hi = sb("p_hi", [P, B, G, N], F16)
        p_lo = sb("p_lo", [P, B, G, N], F16)
        r_den = sb("r_den", [P, B, T, G, HG], F32)
        o32 = sb("o32", [P, B, T, D], F32)
        o_hi = sb("o_hi", [P, B, N], F16)
        o_lo = sb("o_lo", [P, B, N], F16)
        acc = sb("acc", [P, B, T, D], F32)
        zln = sb("zln", [P, B, T, D], F32)
        zT = sb("zT", [P, B, N], F32)
        z_hi = sb("z_hi", [P, B, N], F16)
        z_lo = sb("z_lo", [P, B, N], F16)
        logits = sb("logits", [P, B, T, E], F32)
        r_a = sb("r_a", [P, B, T, E], F32)
        r_b = sb("r_b", [P, B, T, E], F32)
        pick1 = sb("pick1", [P, B, T, E], F32)
        pick2 = sb("pick2", [P, B, T, E], F32)
        top1 = sb("top1", [P, B, T], F32)
        top2 = sb("top2", [P, B, T], F32)
        least = sb("least", [P, B, T], F32)
        gap = sb("gap", [P, B, T], F32)
        th = sb("th", [P, B, T], F32)
        w_1 = sb("w_1", [P, B, T], F32)
        w_2 = sb("w_2", [P, B, T], F32)
        gates = sb("gates", [P, B, T, E], F32)
        gatesT = sb("gatesT", [E, B, N], F32)
        w_scale = sb("w_scale", [P, I], F32)
        unit = sb("unit", [P, I], F32)
        b1_now = sb("b1_now", [P, 2, C], F32)
        raw1 = sb("raw1", [P, 2, I], F32)
        raw2 = sb("raw2", [P, 2, C, D], F32)
        w1_hi = sb("w1_hi", [P, 2, I], F16)
        w1_lo = sb("w1_lo", [P, 2, I], F16)
        w2_hi = sb("w2_hi", [P, 2, C, D], F16)
        w2_lo = sb("w2_lo", [P, 2, C, D], F16)
        h32 = sb("h32", [P, B, C, N], F32)
        h_hi = sb("h_hi", [P, B, C, N], F16)
        h_lo = sb("h_lo", [P, B, C, N], F16)

        ld_x = [sem(f"ld_x{b}") for b in range(B)]
        ld_ctx, ld_wkvo, ld_small, ld_wq, ld_rows, ld_b2 = (
            sem(n) for n in ("ld_ctx", "ld_wkvo", "ld_small", "ld_wq", "ld_rows", "ld_b2"))
        ld_w1 = [sem(f"ld_w1_{i}") for i in range(2)]
        ld_w2 = [sem(f"ld_w2_{i}") for i in range(2)]
        stored = sem("stored")
        consts, pool_step, w_step, hi_step = (sem(n) for n in ("consts", "pool_step", "w_step", "hi_step"))
        wT_ps, smallT_ps, kT_ps, v_ps = (sem(n) for n in ("wT_ps", "smallT_ps", "kT_ps", "v_ps"))
        wT_done, ctxT_done, smallT_done, bq33_done, tanh_done = (
            sem(n) for n in ("wT_done", "ctxT_done", "smallT_done", "bq33_done", "tanh_done"))
        kT_done, kbd_done, kq_ps, bias_row_ps, bias_col_ps = (
            sem(n) for n in ("kT_done", "kbd_done", "kq_ps", "bias_row_ps", "bias_col_ps"))
        kq_hi_done, kq_lo_done, bias_row_done, bias_col_done, v_done, wo_done, v_bank_free = (
            sem(n) for n in ("kq_hi_done", "kq_lo_done", "bias_row_done", "bias_col_done", "v_done", "wo_done",
                             "v_bank_free"))
        dve_step = sem("dve_step")
        xln_done, xT_ps, x_hi_done, x_lo_done = (sem(n) for n in ("xln_done", "xT_ps", "x_hi_done", "x_lo_done"))
        var_done, rstd_done = sem("var_done"), sem("rstd_done")
        scores_ps, max_done, max_split, maxT_ps, maxT_done = (
            sem(n) for n in ("scores_ps", "max_done", "max_split", "maxT_ps", "maxT_done"))
        scoresT_ps, exp_done, p_hi_done, p_lo_done = (
            sem(n) for n in ("scoresT_ps", "exp_done", "p_hi_done", "p_lo_done"))
        pv_ps, o_done, oT_ps, o_hi_done, o_lo_done, attn_ps, x1_done = (
            sem(n) for n in ("pv_ps", "o_done", "oT_ps", "o_hi_done", "o_lo_done", "attn_ps", "x1_done"))
        zln_done, zT_ps, zT_done, z_hi_done, z_lo_done = (
            sem(n) for n in ("zln_done", "zT_ps", "zT_done", "z_hi_done", "z_lo_done"))
        logits_ps, gap_done, th_done, gates_done, gatesT_ps, gatesT_done, b2_ps, acc_ready = (
            sem(n) for n in ("logits_ps", "gap_done", "th_done", "gates_done", "gatesT_ps", "gatesT_done", "b2_ps",
                             "acc_ready"))
        w1_split, w2_split, b1_ready = (sem(n) for n in ("w1_split", "w2_split", "b1_ready"))
        up_ps, gelu_done, h_split, down_ps, acc_done = (
            sem(n) for n in ("up_ps", "gelu_done", "h_split", "down_ps", "acc_done"))

        tok = x.rearrange("b (p t) d -> p b t d", t=T)
        out_tok = out.rearrange("b (p t) d -> p b t d", t=T)
        w1_dram = W1.rearrange("e h i -> h e i")
        w2_dram = W2.rearrange("e (c p) d -> p e c d", p=P)

        wT_bank = bank[0][:, 0:3 * D].rearrange("p (w d) -> p w d", w=3)
        ctxT_bank = bank[1][:, 0:B * M]
        smallT_bank = bank[1][:, B * M:B * M + R_ALL]
        kT_bank = bank[2][:, 0:B * M]
        g_bank = bank[2][:, 64:66]
        bias_col_bank = bank[2][:, 128:128 + B * G]
        v_bank = bank[3][:, 0:B * D].rearrange("p (b d) -> p b d", b=B)
        kq_bank = [bank[4], bank[5]]
        bias_row_bank = [bank[6], bank[7]]
        xT_bank = [bank[0], bank[1]]
        scores_bank = [bank[2], bank[3]]
        scoresT_bank = [bank[4], bank[5]]
        maxT_bank = [bank[6], bank[7]]
        pv_bank = [bank[6], bank[7]]
        oT_bank = [bank[0], bank[1]]
        attn_bank = [bank[2], bank[3]]
        zT_bank = [bank[0], bank[1]]
        logits_bank = [bank[4], bank[5]]
        gatesT_bank = [bank[6], bank[7]]
        b2_bank = [bank[2], bank[3]]
        up_bank = [bank[4], bank[5], bank[6], bank[7]]
        down_bank = [bank[0], bank[1]]

        block = stack.enter_context(nc.Block())

        @block.sync
        def _(sp):
            sp.dma_start(ctx_sb[:, :], ctx_in.rearrange("b m d -> (b m) d")).then_inc(ld_ctx, 16)
            sp.dma_start(wkvo[:, 0, :], Wk).then_inc(ld_wkvo, 16)
            sp.dma_start(x_sb[:, 0], tok[:, 0]).then_inc(ld_x[0], 16)
            sp.dma_start(wq_sb[:, :], Wq).then_inc(ld_wq, 16)
            sp.dma_start(x_sb[:, 1], tok[:, 1]).then_inc(ld_x[1], 16)
            sp.dma_start(b2_sb[:, :], b2).then_inc(ld_b2, 16)
            for e in range(2):
                sp.dma_start(raw1[:, e, :], w1_dram[:, e, :]).then_inc(ld_w1[e], 16)
                sp.dma_start(raw2[:, e], w2_dram[:, e]).then_inc(ld_w2[e], 16)
            with sp.Fori(1, PAIRS) as pair:
                for slot in range(2):
                    e = pair * 2 + slot
                    sp.wait_ge(w1_split, e - 1)
                    sp.dma_start(raw1[:, slot, :], w1_dram[:, bass.ds(e, 1), :].rearrange("h e i -> h (e i)")).then_inc(
                        ld_w1[slot], 16)
                    sp.wait_ge(w2_split, e - 1)
                    sp.dma_start(raw2[:, slot], w2_dram[:, bass.ds(e, 1)].rearrange("p e c d -> p (e c) d")).then_inc(
                        ld_w2[slot], 16)
            for b in range(B):
                sp.wait_ge(acc_done, B * E + b + 1)
                sp.dma_start(out_tok[:, b], acc[:, b]).then_inc(stored, 16)
            sp.wait_ge(stored, 16 * B)

        @block.gpsimd
        def _(pool):
            gp = nc.gpsimd
            gp.memset(ones[:, :], 1.0).then_inc(pool_step, 1)
            gp.memset(head_mask[:, :], K_SCALE * HD ** -0.5).then_inc(pool_step, 1)
            gp.memset(group_mask[:, :, :], 1.0).then_inc(pool_step, 1)
            gp.memset(neg_sel[:, :, :, :], 0.0).then_inc(pool_step, 1)
            gp.memset(ones33[:, :], 1.0).then_inc(consts, 1)
            gp.memset(neg_half[:, :], -0.5).then_inc(consts, 1)
            gp.memset(max_hl[:, :, :, :], 0.0).then_inc(consts, 1)
            gp.memset(bq33[:, :], 0.0).then_inc(consts, 1)
            gp.memset(w_scale[:, :], W_SCALE).then_inc(consts, 1)
            gp.memset(unit[:, :], 1.0).then_inc(consts, 1)
            gp.iota(expert_no[:, :, :], [[0, T], [1, E]], base=0, channel_multiplier=0,
                    allow_small_or_imprecise_dtypes=True).then_inc(consts, 1)
            pool.wait_ge(pool_step, 4)
            gp.affine_select(out=ident[:, :], in_=ones[:, :], pattern=[[-1, P]], compare_op=ALU.is_equal, fill=0.0,
                             base=0, channel_multiplier=1).then_inc(consts, 1)
            gp.affine_select(out=ident_b[:, :], in_=ones[:, :], pattern=[[-1, P]], compare_op=ALU.is_equal, fill=0.0,
                             base=0, channel_multiplier=1).then_inc(consts, 1)
            gp.affine_select(out=head_mask[:, :], in_=head_mask[:, :], pattern=[[-HD, H]], compare_op=ALU.is_ge,
                             fill=0.0, base=0, channel_multiplier=1).then_inc(pool_step, 1)
            gp.affine_select(out=group_mask[:, :, :], in_=group_mask[:, :, :], pattern=[[0, G], [-M, HG]],
                             compare_op=ALU.is_ge, fill=0.0, base=0, channel_multiplier=1).then_inc(pool_step, 1)
            gp.affine_select(out=neg_sel[:, :, :, :], in_=neg_sel[:, :, :, :], pattern=[[-HG, G], [-1, HG], [0, M]],
                             compare_op=ALU.not_equal, fill=-1.0, base=0, channel_multiplier=1).then_inc(pool_step, 1)
            pool.wait_ge(pool_step, 7)
            gp.affine_select(out=head_mask[:, :], in_=head_mask[:, :], pattern=[[HD, H]], compare_op=ALU.is_ge,
                             fill=0.0, base=HD - 1, channel_multiplier=-1).then_inc(consts, 1)
            gp.affine_select(out=group_mask[:, :, :], in_=group_mask[:, :, :], pattern=[[0, G], [M, HG]],
                             compare_op=ALU.is_ge, fill=0.0, base=M - 1, channel_multiplier=-1).then_inc(consts, 1)
            gp.affine_select(out=neg_sel[:, :, :, :], in_=neg_sel[:, :, :, :], pattern=[[-HG, G], [-1, HG], [0, M]],
                             compare_op=ALU.not_equal, fill=-1.0, base=-32, channel_multiplier=1).then_inc(consts, 1)

            pool.wait_ge(consts, 12)
            for n in range(B):
                pool.wait_ge(var_done, n + 1)
                gp.tensor_tensor(rstd[:, n, :], var_eps[:, n, :], neg_half[:, :], ALU.pow).then_inc(rstd_done, 1)


            def split_weights(e, slot):
                pool.wait_ge(ld_w1[slot], 8 * (e - slot) + 16)
                if not isinstance(e, int):
                    pool.wait_ge(gelu_done, B * C * (e - 1))
                gp.tensor_tensor(raw1[:, slot, :], raw1[:, slot, :], w_scale[:, :], ALU.mult).then_inc(w_step, 1)
                gp.tensor_tensor(b1_now[:, slot, :], smallT[:, bass.ds(e * C + R_B1, C)], ones[:, 0:C],
                                 ALU.mult).then_inc(b1_ready, 1)
                pool.wait_ge(w_step, 4 * e + 1)
                gp.tensor_tensor(w1_hi[:, slot, :], raw1[:, slot, :], unit[:, :], ALU.mult).then_inc(w_step, 1)
                pool.wait_ge(w_step, 4 * e + 2)
                gp.tensor_tensor(w1_lo[:, slot, :], raw1[:, slot, :], w1_hi[:, slot, :],
                                 ALU.subtract).then_inc(w1_split, 1)
                pool.wait_ge(ld_w2[slot], 8 * (e - slot) + 16)
                if not isinstance(e, int):
                    pool.wait_ge(down_ps, B * e)
                flat = [w[:, slot].rearrange("p c d -> p (c d)") for w in (raw2, w2_hi, w2_lo)]
                gp.tensor_tensor(flat[0], flat[0], w_scale[:, :], ALU.mult).then_inc(w_step, 1)
                pool.wait_ge(w_step, 4 * e + 3)
                gp.tensor_tensor(flat[1], flat[0], unit[:, :], ALU.mult).then_inc(w_step, 1)
                pool.wait_ge(w_step, 4 * e + 4)
                gp.tensor_tensor(flat[2], flat[0], flat[1], ALU.subtract).then_inc(w2_split, 1)

            pool.wait_ge(smallT_done, 1)
            for e in range(2):
                split_weights(e, e)

            for n in range(B):
                pool.wait_ge(var_done, B + n + 1)
                gp.tensor_tensor(rstd[:, n, :], var_eps[:, n, :], neg_half[:, :], ALU.pow).then_inc(rstd_done, 1)

            with pool.Fori(1, PAIRS) as pair:
                for slot in range(2):
                    split_weights(pair * 2 + slot, slot)

        @block.scalar
        def _(act):
            ac = nc.scalar
            act.dma_start(smalls[R_WG:R_WG + E, :], Wg).then_inc(ld_small, 16)
            act.dma_start(smalls[R_B1:R_B1 + E * C, :], b1.rearrange("e (c i) -> (e c) i", i=P)).then_inc(ld_small, 16)
            act.dma_start(smalls[R_BQ:R_BQ + 1, :], bq.rearrange("(a d) -> a d", a=1)).then_inc(ld_small, 16)
            act.dma_start(smalls[R_BK:R_BK + 1, :], bk.rearrange("(a d) -> a d", a=1)).then_inc(ld_small, 16)
            act.dma_start(wkvo[:, 1, :], Wv).then_inc(ld_wkvo, 16)
            act.dma_start(wkvo[:, 2, :], Wo).then_inc(ld_wkvo, 16)
            act.dma_start(bv_row[:, :], bv.rearrange("(a d) -> a d", a=1)).then_inc(ld_rows, 16)
            act.dma_start(g_row[0:1, 0:1], g_xattn.rearrange("(a d) -> a d", a=1)).then_inc(ld_rows, 16)
            act.dma_start(g_row[0:1, 1:2], g_ffn.rearrange("(a d) -> a d", a=1)).then_inc(ld_rows, 16)

            act.wait_ge(wT_ps, 1)
            ac.copy(wT[:, :, :], wT_bank).then_inc(wT_done, 1)
            act.wait_ge(kT_ps, 1)
            act.wait_ge(smallT_done, 1)
            ac.activation(kT[:, :, :], kT_bank.rearrange("p (b m) -> p b m", b=B), ACT.Identity,
                          bias=smallT[:, R_BK:R_BK + 1]).then_inc(kT_done, 1)
            ac.activation(tanh_g[:, :], g_bank, ACT.Tanh).then_inc(tanh_done, 1)

            def high_half(dst, src, ready, value, done):
                act.wait_ge(ready, value)
                ac.copy(dst, src).then_inc(done, 1)

            high_half(x_hi[:, 0, :], xT_bank[0][:, :], xT_ps, 1, x_hi_done)
            for b in range(B):
                high_half(kq_hi[:, b, :], kq_bank[b][:, :], kq_ps, b + 1, kq_hi_done)
            act.wait_ge(bias_col_ps, 1)
            ac.activation(bias_col[:, :, :], bias_col_bank.rearrange("p (b g) -> p b g", b=B), ACT.Copy,
                          bias=P_LOG_SCALE, scale=1.0 / K_SCALE).then_inc(bias_col_done, 1)
            high_half(x_hi[:, 1, :], xT_bank[1][:, :], xT_ps, 2, x_hi_done)

            for b in range(B):
                act.wait_ge(maxT_ps, b + 1)
                ac.copy(maxT[:, b, :], maxT_bank[b][0:MAX_ROWS, 0:N // 2].bitcast(BF16)).then_inc(maxT_done, 1)
            act.wait_ge(bias_col_done, 1)
            for n in range(B * G):
                b, g = divmod(n, G)
                act.wait_ge(scoresT_ps, n + 1)
                if n >= 2:
                    act.wait_ge(p_lo_done, n - 1)
                ac.activation(p32[:, n % 2, :], scoresT_bank[n % 2][:, :], ACT.Exp, bias=bias_col[:, b, g:g + 1],
                              scale=1.0 / K_SCALE).then_inc(exp_done, 1)
                act.wait_ge(exp_done, n + 1)
                ac.copy(p_hi[:, b, g, :], p32[:, n % 2, :]).then_inc(p_hi_done, 1)
            for b in range(B):
                high_half(o_hi[:, b, :], oT_bank[b][:, :], oT_ps, b + 1, o_hi_done)
            for b in range(B):
                act.wait_ge(zT_ps, b + 1)
                ac.copy(zT[:, b, :], zT_bank[b][:, :]).then_inc(zT_done, 1)
                ac.copy(z_hi[:, b, :], zT_bank[b][:, :]).then_inc(z_hi_done, 1)
            for b in range(B):
                act.wait_ge(gap_done, b + 1)
                ac.activation(th[:, b, :], gap[:, b, :], ACT.Tanh, scale=0.5).then_inc(th_done, 1)

            with act.Fori(0, PAIRS) as pair:
                for k in range(4):
                    s = pair * 4 + k
                    e, b = pair * 2 + k // 2, k % 2
                    if b == 0:
                        act.wait_ge(b1_ready, e + 1)
                    act.wait_ge(h_split, 2 * s + 2)
                    for c in range(C):
                        act.wait_ge(up_ps, C * s + c + 1)
                        ac.activation(h32[:, b, c, :], up_bank[c][:, :], ACT.Gelu,
                                      bias=b1_now[:, k // 2, c:c + 1],
                                      scale=1.0 / W_SCALE).then_inc(gelu_done, 1)

        @block.tensor
        def _(pe):
            te = nc.tensor

            def product(out_, a_hi, a_lo, b_hi, b_lo, start=True, stop=True):
                te.matmul(out_, a_hi, b_hi, start=start, stop=False, skip_group_check=True)
                te.matmul(out_, a_hi, b_lo, start=False, stop=False, skip_group_check=True)
                return te.matmul(out_, a_lo, b_hi, start=False, stop=stop, skip_group_check=True)

            pe.wait_ge(consts, 12)
            pe.wait_ge(ld_ctx, 16)
            te.transpose(ctxT_bank, ctx_sb[:, :], ident[0:B * M, 0:B * M])
            pe.wait_ge(ld_small, 64)
            te.transpose(smallT_bank, smalls[:, :], ident[0:R_ALL, 0:R_ALL]).then_inc(smallT_ps, 1)
            pe.wait_ge(ld_wkvo, 48)
            for w in range(3):
                t_ = te.transpose(wT_bank[:, w, :], wkvo[:, w, :], ident[:, :])
            t_.then_inc(wT_ps, 1)
            pe.wait_ge(ld_rows, 48)
            te.matmul(g_bank, ones[0:1, :], g_row[:, :], start=True, stop=True)
            pe.wait_ge(wT_done, 1)
            pe.wait_ge(ctxT_done, 1)
            te.matmul(kT_bank, wT[:, 0, :], ctxT[:, :], start=True, stop=True).then_inc(kT_ps, 1)
            for b in range(B):
                te.matmul(v_bank[:, b, :], ctxT4[:, b].rearrange("p h m -> p (h m)"), wT[:, 1, :], start=True,
                          stop=False)
                t_ = te.matmul(v_bank[:, b, :], ones[0:1, :], bv_row[:, :], start=False, stop=True)
            t_.then_inc(v_ps, 1)

            def transpose_x(b):
                pe.wait_ge(xln_done, b + 1)
                for t in range(T):
                    t_ = te.transpose(xT_bank[b][:, t * P:(t + 1) * P], xln[:, b, t, :], ident[:, :])
                t_.then_inc(xT_ps, 1)

            transpose_x(0)
            pe.wait_ge(ld_wq, 16)
            pe.wait_ge(kbd_done, 1)
            for b in range(B):
                te.matmul(kq_bank[b][:, :], wq_sb[:, :], k_bd[:, b].rearrange("p h m -> p (h m)"), start=True,
                          stop=True).then_inc(kq_ps, 1)
            pe.wait_ge(bq33_done, 1)
            for b in range(B):
                te.matmul(bias_row_bank[b][0:BIAS_ROWS, :], bq33[:, :], k_bd[:, b].rearrange("p h m -> p (h m)"),
                          start=True, stop=True).then_inc(bias_row_ps, 1)
            pe.wait_ge(tanh_done, 1)
            for b in range(B):
                for g in range(G):
                    t_ = te.matmul(bias_col_bank[:, b * G + g:b * G + g + 1],
                                   k_bd[:, b, g * HG:(g + 1) * HG].rearrange("p h m -> p (h m)"), bq33[:, 0:1],
                                   start=True, stop=True)
            t_.then_inc(bias_col_ps, 1)
            transpose_x(1)
            pe.wait_ge(bias_col_done, 1)
            pe.wait_ge(v_bank_free, 1)

            for b in range(B):
                pe.wait_ge(x_hi_done, b + 1)
                pe.wait_ge(x_lo_done, b + 1)
                pe.wait_ge(kq_hi_done, b + 1)
                pe.wait_ge(kq_lo_done, b + 1)
                pe.wait_ge(bias_row_done, b + 1)
                for t in range(T):
                    n = b * T + t
                    if n >= 2:
                        pe.wait_ge(max_done, n - 1)
                    rows = slice(t * P, (t + 1) * P)
                    product(scores_bank[n % 2][:, :], x_hi[:, b, rows], x_lo[:, b, rows], kq_hi[:, b, :],
                            kq_lo[:, b, :], stop=False)
                    te.matmul(scores_bank[n % 2][:, :], ones33[:, :], bias33[:, b, :], start=False, stop=True,
                              skip_group_check=True).then_inc(scores_ps, 1)
            for b in range(B):
                pe.wait_ge(max_split, b + 1)
                for t in range(T):
                    t_ = te.transpose(maxT_bank[b][0:MAX_ROWS, t * P // 2:(t + 1) * P // 2].bitcast(BF16),
                                      max_hl[:, b, t, :], ident_b[:, :])
                t_.then_inc(maxT_ps, 1)
            for n in range(B * G):
                b, g = divmod(n, G)
                if g == 0:
                    pe.wait_ge(maxT_done, b + 1)
                if n >= 2:
                    pe.wait_ge(exp_done, n - 1)
                rows = slice(g * P, (g + 1) * P)
                product(scoresT_bank[n % 2][:, :], kq_hi[:, b, rows], kq_lo[:, b, rows], x_hi[:, b, :], x_lo[:, b, :],
                        stop=False)
                te.matmul(scoresT_bank[n % 2][:, :], neg_sel[:, g].rearrange("p h m -> p (h m)"), maxT[:, b, :],
                          start=False, stop=True, skip_group_check=True).then_inc(scoresT_ps, 1)
            pe.wait_ge(v_done, 1)
            for b in range(B):
                pe.wait_ge(p_hi_done, (b + 1) * G)
                pe.wait_ge(p_lo_done, (b + 1) * G)
                for half in range(2):
                    if b > 0:
                        pe.wait_ge(o_done, 2 * (b - 1) + half + 1)
                    for u in range(2):
                        t = 2 * half + u
                        rows = slice(t * P, (t + 1) * P)
                        for g in range(G):
                            at = (u * G + g) * VC
                            first = u == 0 and g == 0
                            last = u == 1 and g == G - 1
                            full = pv_bank[half][:, at:at + VC]
                            te.matmul(full, p_hi[:, b, g, rows], vr[:, b, g, :], start=first, stop=False,
                                      skip_group_check=True)
                            te.matmul(full[:, 0:HG * HD], p_hi[:, b, g, rows], v_lo[:, b, g, :], start=False,
                                      stop=False, skip_group_check=True)
                            t_ = te.matmul(full, p_lo[:, b, g, rows], vr[:, b, g, :], start=False, stop=last,
                                           skip_group_check=True)
                    t_.then_inc(pv_ps, 1)
            for b in range(B):
                for t in range(T):
                    if t % 2 == 0:
                        pe.wait_ge(o_done, 2 * b + t // 2 + 1)
                    t_ = te.transpose(oT_bank[b][:, t * P:(t + 1) * P], o32[:, b, t, :], ident[:, :])
                t_.then_inc(oT_ps, 1)
            pe.wait_ge(wo_done, 1)
            for b in range(B):
                pe.wait_ge(o_hi_done, b + 1)
                pe.wait_ge(o_lo_done, b + 1)
                for t in range(T):
                    rows = slice(t * P, (t + 1) * P)
                    t_ = product(attn_bank[b][:, rows], o_hi[:, b, rows], o_lo[:, b, rows], wo_hi[:, :], wo_lo[:, :],
                                 start=(t == 0), stop=(t == T - 1))
                t_.then_inc(attn_ps, 1)
            for b in range(B):
                pe.wait_ge(zln_done, b + 1)
                for t in range(T):
                    t_ = te.transpose(zT_bank[b][:, t * P:(t + 1) * P], zln[:, b, t, :], ident[:, :])
                t_.then_inc(zT_ps, 1)
            for b in range(B):
                pe.wait_ge(zT_done, b + 1)
                for t in range(T):
                    t_ = te.matmul(logits_bank[b][:, t * E:(t + 1) * E], zT[:, b, t * P:(t + 1) * P],
                                   smallT[:, R_WG:R_WG + E], start=True, stop=True)
                t_.then_inc(logits_ps, 1)
            for b in range(B):
                pe.wait_ge(gates_done, b + 1)
                for t in range(T):
                    t_ = te.transpose(gatesT_bank[b][0:E, t * P:(t + 1) * P], gates[:, b, t, :], ident[:, :])
                t_.then_inc(gatesT_ps, 1)
            for b in range(B):
                pe.wait_ge(gatesT_done, b + 1)
                for t in range(T):
                    t_ = te.matmul(b2_bank[b][:, t * P:(t + 1) * P], gatesT[:, b, t * P:(t + 1) * P], b2_scaled[:, :],
                                   start=True, stop=True)
                t_.then_inc(down_ps, 1)

            def up(s, slot, b, first=False):
                for c in range(C):
                    cols = slice(c * P, (c + 1) * P)
                    if not first:
                        pe.wait_ge(gelu_done, C * (s - 1) + c + 1)
                    t_ = product(up_bank[c][:, :], w1_hi[:, slot, cols], w1_lo[:, slot, cols], z_hi[:, b, :],
                                 z_lo[:, b, :])
                    t_.then_inc(up_ps, 1)

            def down(s, slot, b):
                pe.wait_ge(acc_done, s + 1)
                for c in range(C):
                    if c % 2 == 0:
                        pe.wait_ge(h_split, 2 * s + c // 2 + 5)
                    for t in range(T):
                        rows = slice(t * P, (t + 1) * P)
                        t_ = product(down_bank[b][:, rows], h_hi[:, b, c, rows], h_lo[:, b, c, rows],
                                     w2_hi[:, slot, c, :], w2_lo[:, slot, c, :], start=(c == 0 and t == 0),
                                     stop=(c == C - 1 and t == T - 1))
                t_.then_inc(down_ps, 1)
                return t_

            for b in range(B):
                pe.wait_ge(z_hi_done, b + 1)
            pe.wait_ge(h_split, 2 * B)
            pe.wait_ge(w1_split, 1)
            up(0, 0, 0, first=True)

            def turn(pair, last=False):
                for k in range(4):
                    s = pair * 4 + k
                    if k < 3 or not last:
                        slot_next, b_next = ((k + 1) // 2) % 2, (k + 1) % 2
                        if b_next == 0:
                            pe.wait_ge(w1_split, pair * 2 + (k + 1) // 2 + 1)
                        up(s + 1, slot_next, b_next)
                    if k % 2 == 0:
                        pe.wait_ge(w2_split, pair * 2 + k // 2 + 1)
                    down(s, k // 2, k % 2)

            with pe.Fori(0, PAIRS - 1) as pair:
                turn(pair)
            turn(PAIRS - 1, last=True)

        @block.vector
        def _(dve):
            ve = nc.vector
            count = [0]

            def link(ins):
                count[0] += 1
                ins.then_inc(dve_step, 1)
                dve.wait_ge(dve_step, count[0])

            def moments_of(src, b):
                for t in range(T):
                    i_ = ve.bn_stats(stats[:, b, t, :], src[:, b, t, :])
                link(i_)
                for t in range(T):
                    i_ = ve.bn_aggr(moments[:, b, t, :], stats[:, b, t, :])
                link(i_)
                ve.tensor_scalar(var_eps[:, b, :], moments[:, b, :, 1], LN_EPS, None, ALU.add).then_inc(var_done, 1)

            def normalise(dst, src, b, value, done):
                dve.wait_ge(rstd_done, value)
                for t in range(T):
                    i_ = ve.tensor_scalar(dst[:, b, t, :], src[:, b, t, :], moments[:, b, t, 0:1],
                                          rstd[:, b, t:t + 1], ALU.subtract, ALU.mult)
                i_.then_inc(done, 1)

            dve.wait_ge(ld_x[0], 16)
            moments_of(x_sb, 0)
            dve.wait_ge(smallT_ps, 1)
            ve.tensor_copy(ctxT[:, :], ctxT_bank)
            for b in range(B):
                for h in range(HG):
                    ve.tensor_copy(ctxT4[:, b, h, :], ctxT_bank[:, b * M:(b + 1) * M])
            ve.tensor_copy(smallT[:, :], smallT_bank).then_inc(ctxT_done, 1)
            dve.wait_ge(ctxT_done, 1)
            dve.wait_ge(consts, 12)
            ve.tensor_copy(bq33[:, 0:1], smallT[:, R_BQ:R_BQ + 1]).then_inc(smallT_done, 1)
            ve.tensor_copy(bq33[:, 32:33], smallT[:, R_BQ:R_BQ + 1]).then_inc(bq33_done, 1)
            normalise(xln, x_sb, 0, 1, xln_done)
            dve.wait_ge(ld_x[1], 16)
            moments_of(x_sb, 1)
            dve.wait_ge(kT_done, 1)
            for b in range(B):
                i_ = ve.tensor_tensor(k_bd[:, b], kT[:, b, :].unsqueeze(1).to_broadcast([P, H, M]),
                                      head_mask[:, :].unsqueeze(2).to_broadcast([P, H, M]), ALU.mult)
            i_.then_inc(kbd_done, 1)
            normalise(xln, x_sb, 1, 2, xln_done)

            def low_half(dst, src, high, done, value):
                dve.wait_ge(done, value)
                return ve.tensor_tensor(dst, src, high, ALU.subtract)

            low_half(x_lo[:, 0, :], xT_bank[0][:, :], x_hi[:, 0, :], x_hi_done, 1).then_inc(x_lo_done, 1)
            for b in range(B):
                low_half(kq_lo[:, b, :], kq_bank[b][:, :], kq_hi[:, b, :], kq_hi_done, b + 1).then_inc(kq_lo_done, 1)
                dve.wait_ge(bias_row_ps, b + 1)
                link(ve.tensor_copy(bias33[:, b, :], bias_row_bank[b][0:BIAS_ROWS, :]))
                ve.tensor_tensor(bias33[32:33, b, :], bias_row_bank[b][32:33, :], bias33[32:33, b, :],
                                 ALU.subtract).then_inc(bias_row_done, 1)
                if b == 0:
                    dve.wait_ge(v_ps, 1)
                    for bb in range(B):
                        i_ = ve.tensor_tensor(
                            v32[:, bb, :].rearrange("p (g h d) -> p (g h) d", g=G, h=HG),
                            v_bank[:, bb, :].rearrange("p (g h d) -> p (g h) d", g=G, h=HG),
                            group_mask[:, :, :].rearrange("p g h -> p (g h)").unsqueeze(2).to_broadcast([P, H, HD]),
                            ALU.mult)
                    i_.then_inc(v_bank_free, 1)
            low_half(x_lo[:, 1, :], xT_bank[1][:, :], x_hi[:, 1, :], x_hi_done, 2).then_inc(x_lo_done, 1)

            def split_maxima(b):
                link(ve.tensor_copy(max_hl[:, b, :, 0:H], maxes[:, b, :, :]))
                ve.tensor_tensor(max_hl[:, b, :, 32:32 + H], maxes[:, b, :, :], max_hl[:, b, :, 0:H],
                                 ALU.subtract).then_inc(max_split, 1)

            for b in range(B):
                for t in range(T):
                    n = b * T + t
                    dve.wait_ge(scores_ps, n + 1)
                    ve.tensor_reduce(maxes[:, b, t, :], scores_bank[n % 2][:, :].rearrange("p (h m) -> p h m", h=H),
                                     AX.X, ALU.max).then_inc(max_done, 1)
                dve.wait_ge(max_done, T * (b + 1))
                split_maxima(b)

            dve.wait_ge(v_bank_free, 1)
            for b in range(B):
                v_ = v32[:, b, :].rearrange("p (g c) -> p g c", g=G)
                ve.tensor_scalar(vr[:, b, :, HG * HD:VC], group_mask[:, :, :], 1.0 / O_SCALE, None, ALU.mult)
                link(ve.tensor_copy(vr[:, b, :, 0:HG * HD], v_))
                i_ = ve.tensor_tensor(v_lo[:, b, :, :], v_, vr[:, b, :, 0:HG * HD], ALU.subtract)
            i_.then_inc(v_done, 1)
            dve.wait_ge(tanh_done, 1)
            dve.wait_ge(wT_done, 1)
            link(ve.tensor_scalar(wo32[:, :], wT[:, 2, :], tanh_g[:, 0:1], WO_SCALE, ALU.mult, ALU.mult))
            link(ve.tensor_copy(wo_hi[:, :], wo32[:, :]))
            ve.tensor_tensor(wo_lo[:, :], wo32[:, :], wo_hi[:, :], ALU.subtract).then_inc(wo_done, 1)
            ve.tensor_scalar(half_gate[:, 0:1], tanh_g[:, 1:2], 0.5 * GATE_SCALE, None, ALU.mult)
            ve.tensor_scalar(half_gate[:, 1:2], tanh_g[:, 1:2], -0.5 * GATE_SCALE, None, ALU.mult)
            dve.wait_ge(ld_b2, 16)
            link(ve.tensor_scalar(b2_scaled[:, :], b2_sb[:, :], 1.0 / GATE_SCALE, None, ALU.mult))

            def normalise_heads(b, half):
                dve.wait_ge(pv_ps, 2 * b + half + 1)
                sums = pv_bank[half][:, 0:2 * G * VC].rearrange("p (u c) -> p u c", c=VC)
                r_ = r_den[:, b, 2 * half:2 * half + 2].rearrange("p t g h -> p (t g) h")
                link(ve.reciprocal(r_, sums[:, :, HG * HD:VC]))
                ve.tensor_tensor(
                    o32[:, b, 2 * half:2 * half + 2, :].rearrange("p t (g h d) -> p (t g) h d", g=G, h=HG),
                    sums[:, :, 0:HG * HD].rearrange("p u (h d) -> p u h d", h=HG),
                    r_.unsqueeze(3).to_broadcast([P, 2 * G, HG, HD]), ALU.mult).then_inc(o_done, 1)

            for n in range(B * G):
                b, g = divmod(n, G)
                dve.wait_ge(p_hi_done, n + 1)
                ve.tensor_tensor(p_lo[:, b, g, :], p32[:, n % 2, :], p_hi[:, b, g, :],
                                 ALU.subtract).then_inc(p_lo_done, 1)
            for b in range(B):
                for half in range(2):
                    normalise_heads(b, half)
            for b in range(B):
                low_half(o_lo[:, b, :], oT_bank[b][:, :], o_hi[:, b, :], o_hi_done, b + 1).then_inc(o_lo_done, 1)
            for b in range(B):
                dve.wait_ge(attn_ps, b + 1)
                link(ve.scalar_tensor_tensor(
                    out=acc[:, b].rearrange("p t d -> p (t d)"), in0=attn_bank[b][:, :],
                    scalar=1.0 / (O_SCALE * WO_SCALE), in1=x_sb[:, b].rearrange("p t d -> p (t d)"), op0=ALU.mult,
                    op1=ALU.add))
                moments_of(acc, b)
            for b in range(B):
                normalise(zln, acc, b, B + b + 1, zln_done)
            for b in range(B):
                low_half(z_lo[:, b, :], zT_bank[b][:, :], z_hi[:, b, :], z_hi_done, b + 1).then_inc(h_split, 2)

            def wide(ap):
                return ap.unsqueeze(2).to_broadcast([P, T, E])

            def first_of(b, values, top, pick):
                link(ve.tensor_reduce(top[:, b, :], values, AX.X, ALU.max))
                link(ve.tensor_tensor(r_a[:, b], values, wide(top[:, b, :]), ALU.is_equal))
                link(ve.scalar_tensor_tensor(out=r_b[:, b], in0=r_a[:, b], scalar=-float(E), in1=expert_no[:, :, :],
                                             op0=ALU.mult, op1=ALU.add))
                link(ve.tensor_reduce(least[:, b, :], r_b[:, b], AX.X, ALU.min))
                link(ve.tensor_tensor(pick[:, b], r_b[:, b], wide(least[:, b, :]), ALU.is_equal))

            for b in range(B):
                dve.wait_ge(logits_ps, b + 1)
                link(ve.tensor_copy(logits[:, b].rearrange("p t e -> p (t e)"), logits_bank[b][:, 0:T * E]))
                first_of(b, logits[:, b], top1, pick1)
                link(ve.scalar_tensor_tensor(out=logits[:, b], in0=pick1[:, b], scalar=MASKED, in1=logits[:, b],
                                             op0=ALU.mult, op1=ALU.add))
                first_of(b, logits[:, b], top2, pick2)
                ve.tensor_tensor(gap[:, b, :], top1[:, b, :], top2[:, b, :], ALU.subtract).then_inc(gap_done, 1)
            for b in range(B):
                dve.wait_ge(th_done, b + 1)
                ve.tensor_scalar(w_1[:, b, :], th[:, b, :], 1.0, half_gate[:, 0:1], ALU.add, ALU.mult)
                link(ve.tensor_scalar(w_2[:, b, :], th[:, b, :], -1.0, half_gate[:, 1:2], ALU.add, ALU.mult))
                ve.tensor_tensor(pick1[:, b], pick1[:, b], wide(w_1[:, b, :]), ALU.mult)
                link(ve.tensor_tensor(pick2[:, b], pick2[:, b], wide(w_2[:, b, :]), ALU.mult))
                ve.tensor_tensor(gates[:, b], pick1[:, b], pick2[:, b], ALU.add).then_inc(gates_done, 1)
            for b in range(B):
                dve.wait_ge(gatesT_ps, b + 1)
                ve.tensor_copy(gatesT[:, b, :], gatesT_bank[b][0:E, :]).then_inc(gatesT_done, 1)
            for b in range(B):
                dve.wait_ge(down_ps, b + 1)
                acc_ = acc[:, b].rearrange("p t d -> p (t d)")
                ve.tensor_tensor(acc_, b2_bank[b][:, :], acc_, ALU.add).then_inc(acc_done, 1)

            def split_hidden(s, b):
                dve.wait_ge(down_ps, s + 1)
                for j in range(2):
                    pair_ = slice(2 * j, 2 * j + 2)
                    dve.wait_ge(gelu_done, C * s + 2 * j + 2)
                    ve.tensor_scalar(h_hi[:, b, pair_, :], h32[:, b, pair_, :], H_SCALE, None,
                                     ALU.mult).then_inc(hi_step, 1)
                    dve.wait_ge(hi_step, 2 * s + j + 1)
                    ve.scalar_tensor_tensor(out=h_lo[:, b, pair_, :], in0=h32[:, b, pair_, :], scalar=H_SCALE,
                                            in1=h_hi[:, b, pair_, :], op0=ALU.mult,
                                            op1=ALU.subtract).then_inc(h_split, 1)

            def accumulate(s, e, b):
                dve.wait_ge(down_ps, s + 3)
                dve.wait_ge(acc_done, s + 1)
                for t in range(T):
                    i_ = ve.scalar_tensor_tensor(
                        out=acc[:, b, t, :], in0=down_bank[b][:, t * P:(t + 1) * P],
                        scalar=gates[:, b, t, bass.ds(e, 1)], in1=acc[:, b, t, :], op0=ALU.mult, op1=ALU.add)
                i_.then_inc(acc_done, 1)

            dve.wait_ge(gates_done, B)
            split_hidden(0, 0)

            def turn(pair, last=False):
                for k in range(4):
                    s = pair * 4 + k
                    if k < 3 or not last:
                        split_hidden(s + 1, (k + 1) % 2)
                    accumulate(s, pair * 2 + k // 2, k % 2)

            with dve.Fori(0, PAIRS - 1) as pair:
                turn(pair)
            turn(PAIRS - 1, last=True)


INS = ["x", "ctx_1024", "g_xattn", "g_ffn", "L0_xattn_Wq", "L0_xattn_bq", "L0_xattn_Wk", "L0_xattn_bk", "L0_xattn_Wv",
       "L0_xattn_bv", "L0_xattn_Wo", "L0_ffn_Wg", "L0_ffn_W1", "L0_ffn_b1", "L0_ffn_W2", "L0_ffn_b2"]


def kernel(**inputs):
    import numpy as np
    import concourse.bacc as bacc
    from concourse.bass_utils import run_bass_kernel_spmd

    nc = bacc.Bacc("TRN2", target_bir_lowering=False, num_devices=1)
    arrays, args = {}, []
    for name in INS:
        a = np.ascontiguousarray(inputs[name])
        arrays[name] = a
        args.append(nc.dram_tensor(name, a.shape, mybir.dt.from_np(a.dtype), kind="ExternalInput").ap())
    out = nc.dram_tensor("out", arrays["x"].shape, F32, kind="ExternalOutput").ap()
    gated_block(nc, *args, out)
    r = run_bass_kernel_spmd(nc, [arrays], core_ids=[0])
    return r.results[0]["out"]
```

```python
from contextlib import ExitStack

import concourse.bass as bass
from concourse import mybir

ALU = mybir.AluOpType
ACT = mybir.ActivationFunctionType
AX = mybir.AxisListType
F32 = mybir.dt.float32
F16 = mybir.dt.float16
BF16 = mybir.dt.bfloat16

LN_EPS = 1e-5
K_SCALE = 16.0
P_LOG_SCALE = 5.545177444479562
GATE_SCALE = 16.0
B2_SCALE = 16.0
O_SCALE = 16.0
WO_SCALE = 16.0
W_SCALE = 256.0
H_SCALE = 16.0
MASKED = -3.0e38


def gated_block(nc, x, ctx_in, g_xattn, g_ffn, Wq, bq, Wk, bk, Wv, bv, Wo, Wg, W1, b1, W2, b2, out):
    B, N, D = x.shape
    M = ctx_in.shape[1]
    H = 16
    HD = D // H
    E, _, I = W1.shape
    P = 128
    T = N // P
    G = H * M // P
    HG = H // G
    C = I // P
    VC = HG * HD + HG
    BIAS_ROWS = 33
    MAX_ROWS = 32 + H
    GATE_ROWS = 32 + E
    assert (B, N, D, M, E, I) == (2, 512, 128, 32, 8, 512)
    R_WG, R_B1, R_ALL = 0, E, E + E * C
    C_SMALL = 2 * D
    DVE_ADDS = 3
    S = B * E

    with ExitStack() as stack:
        def sb(name, shape, dt):
            return stack.enter_context(nc.sbuf_tensor(name, shape, dt))

        def sem(name):
            return stack.enter_context(nc.semaphore(name))

        bank = [stack.enter_context(nc.psum_tensor(f"bank{i}", [P, 512], F32)) for i in range(8)]

        ones = sb("ones", [P, P], F32)
        ident = sb("ident", [P, P], F32)
        ident_b = sb("ident_b", [P, P], BF16)
        ones33 = sb("ones33", [BIAS_ROWS, P], F16)
        head_mask = sb("head_mask", [P, H], F32)
        group_mask = sb("group_mask", [P, G, HG], F32)
        neg_sel = sb("neg_sel", [MAX_ROWS, G, HG, M], BF16)
        expert_no = sb("expert_no", [P, T, E], F32)
        pick_expert = sb("pick_expert", [GATE_ROWS, E * P], F16)
        ident_h = sb("ident_h", [P, P], F16)
        x_sb = sb("x_sb", [P, B, T, D], F32)
        ctx_sb = sb("ctx_sb", [B * M, D], F32)
        wk_sb = sb("wk_sb", [P, D], F32)
        wvo_sb = sb("wvo_sb", [P, 2, D], F32)
        wq_sb = sb("wq_sb", [P, D], F32)
        smalls = sb("smalls", [R_ALL, D], F32)
        qkv_rows = sb("qkv_rows", [1, 3, D], F32)
        g_row = sb("g_row", [1, 2], F32)
        b2_sb = sb("b2_sb", [GATE_ROWS, D], F32)
        wkT = sb("wkT", [P, D], F32)
        turned = sb("turned", [P, C_SMALL + R_ALL], F32)
        wvT, woT, smallT = turned[:, 0:D], turned[:, D:2 * D], turned[:, C_SMALL:C_SMALL + R_ALL]
        ctxT = sb("ctxT", [P, B * M], F32)
        ctxT4 = sb("ctxT4", [P, B, HG, M], F32)
        sel33 = sb("sel33", [1, BIAS_ROWS], F32)
        bq33 = sb("bq33", [P, BIAS_ROWS], F32)
        tanh_g = sb("tanh_g", [P, 2], F32)
        gelu_first = sb("gelu_first", [P, 1], F32)
        half_gate = sb("half_gate", [P, 2], F32)
        b2_hi = sb("b2_hi", [GATE_ROWS, D], F16)
        b2_lo = sb("b2_lo", [GATE_ROWS, D], F16)
        wo32 = sb("wo32", [P, D], F32)
        wo_hi = sb("wo_hi", [P, D], F16)
        wo_lo = sb("wo_lo", [P, D], F16)
        k_bd = sb("k_bd", [P, B, H, M], F32)
        kq_hi = sb("kq_hi", [P, B, H * M], F16)
        kq_lo = sb("kq_lo", [P, B, H * M], F16)
        bias33 = sb("bias33", [BIAS_ROWS, B, H * M], F16)
        bias_col = sb("bias_col", [P, B, G], F32)
        v32 = sb("v32", [P, B, D], F32)
        vr = sb("vr", [P, B, G, VC], F16)
        v_lo = sb("v_lo", [P, B, G, HG * HD], F16)
        stats = sb("stats", [P, B, T, 6], F32)
        moments = sb("moments", [P, B, T, 2], F32)
        rstd = sb("rstd", [P, B, T], F32)
        neg_half = sb("neg_half", [P, T], F32)
        var_eps = sb("var_eps", [P, B, T], F32)
        xln = sb("xln", [P, B, T, D], F32)
        x_hi = sb("x_hi", [P, B, N], F16)
        x_lo = sb("x_lo", [P, B, N], F16)
        maxes = sb("maxes", [P, B, T, H], F32)
        max_hl = sb("max_hl", [P, B, T, MAX_ROWS], BF16)
        maxT = sb("maxT", [MAX_ROWS, B, N], BF16)
        p32 = sb("p32", [P, B, G, N], F32)
        p_hi = sb("p_hi", [P, B, G, N], F16)
        p_lo = sb("p_lo", [P, B, G, N], F16)
        r_den = sb("r_den", [P, B, T, G, HG], F32)
        o32 = xln
        o_hi = sb("o_hi", [P, B, N], F16)
        o_lo = sb("o_lo", [P, B, N], F16)
        x1 = sb("x1", [P, B, T, D], F32)
        zln = xln
        zT = k_bd[:, :, :, :].rearrange("p b h m -> p b (h m)")
        z_hi = sb("z_hi", [P, B, N], F16)
        z_lo = sb("z_lo", [P, B, N], F16)
        logits = sb("logits", [P, B, T, E], F32)
        r_a = sb("r_a", [P, B, T, E], F32)
        r_b = sb("r_b", [P, B, T, E], F32)
        pick1 = sb("pick1", [P, B, T, E], F32)
        pick2 = sb("pick2", [P, B, T, E], F32)
        top1 = sb("top1", [P, B, T], F32)
        top2 = sb("top2", [P, B, T], F32)
        least = sb("least", [P, B, T], F32)
        gap = sb("gap", [P, B, T], F32)
        th = sb("th", [P, B, T], F32)
        w_1 = sb("w_1", [P, B, T], F32)
        w_2 = sb("w_2", [P, B, T], F32)
        gates = sb("gates", [P, B, T, E], F32)
        gates_hl = sb("gates_hl", [P, B, T, GATE_ROWS], F16)
        gatesT = sb("gatesT", [GATE_ROWS, B, N], F16)
        w_scale = sb("w_scale", [P, I], F32)
        unit = sb("unit", [P, I], F32)
        raw1 = sb("raw1", [P, E, I], F32)
        raw2 = sb("raw2", [P, E, C * D], F32)
        w1_hi = sb("w1_hi", [P, E * I], F16)
        w1_lo = sb("w1_lo", [P, E * I], F16)
        w2_hi = sb("w2_hi", [P, E * C * D], F16)
        w2_lo = sb("w2_lo", [P, E * C * D], F16)
        gate_all = sb("gate_all", [P, E, N], F32)
        gate_now = gate_all
        h32 = [p32[:, 0], sb("h32", [P, C, N], F32)]
        h_hi = sb("h_hi", [P, 2, C, N], F16)
        h_lo = sb("h_lo", [P, 2, C, N], F16)
        gated = sb("gated", [P, 2, N], F32)
        accT = sb("accT", [P, B, N], F32)
        out_sb = xln

        ld_x = [sem(f"ld_x{b}") for b in range(B)]
        ld_ctx, ld_wk, ld_wvo, ld_small, ld_wq, ld_bk, ld_bq, ld_bv, ld_g, ld_b2 = (
            sem(n) for n in ("ld_ctx", "ld_wk", "ld_wvo", "ld_small", "ld_wq", "ld_bk", "ld_bq", "ld_bv", "ld_g",
                             "ld_b2"))
        ld_w = [sem(f"ld_w{e}") for e in range(E)]
        stored = sem("stored")
        pool_step, w_step, max_consts, neg_sel_done, group_mask_done, gate_consts = (
            sem(n) for n in ("pool_step", "w_step", "max_consts", "neg_sel_done", "group_mask_done", "gate_consts"))
        wkT_ps, ctxT_ps, bq33_ps, turned_ps, kT_ps, v_ps, g_ps = (
            sem(n) for n in ("wkT_ps", "ctxT_ps", "bq33_ps", "turned_ps", "kT_ps", "v_ps", "g_ps"))
        ident_done, head_mask_done, sel33_done, ones33_done = (
            sem(n) for n in ("ident_done", "head_mask_done", "sel33_done", "ones33_done"))
        wkT_done, ctxT_done, ctxT4_done, bq33_done, turned_done, tanh_done = (
            sem(n) for n in ("wkT_done", "ctxT_done", "ctxT4_done", "bq33_done", "turned_done", "tanh_done"))
        kbd_done, kq_ps, bias_row_ps, bias_col_ps = (
            sem(n) for n in ("kbd_done", "kq_ps", "bias_row_ps", "bias_col_ps"))
        kq_hi_done, kq_lo_done, bias_hi_done, bias_lo_done, bias_col_done, v_done, wo_done = (
            sem(n) for n in ("kq_hi_done", "kq_lo_done", "bias_hi_done", "bias_lo_done", "bias_col_done", "v_done",
                             "wo_done"))
        dve_step = sem("dve_step")
        xln_done, xT_ps, x_hi_done, x_lo_done = (sem(n) for n in ("xln_done", "xT_ps", "x_hi_done", "x_lo_done"))
        var_done, rstd_done = sem("var_done"), sem("rstd_done")
        scores_ps, max_done, max_split, maxT_ps, maxT_done = (
            sem(n) for n in ("scores_ps", "max_done", "max_split", "maxT_ps", "maxT_done"))
        scoresT_ps, exp_done, p_hi_done, p_lo_done = (
            sem(n) for n in ("scoresT_ps", "exp_done", "p_hi_done", "p_lo_done"))
        pv_ps, o_done, oT_ps, o_hi_done, o_lo_done, attn_ps, x1_done = (
            sem(n) for n in ("pv_ps", "o_done", "oT_ps", "o_hi_done", "o_lo_done", "attn_ps", "x1_done"))
        zln_done, zT_ps, zT_done, z_hi_done, z_lo_done = (
            sem(n) for n in ("zln_done", "zT_ps", "zT_done", "z_hi_done", "z_lo_done"))
        logits_ps, logits_done, gap_done, th_done, gates_done, gatesT_ps, gatesT_done = (
            sem(n) for n in ("logits_ps", "logits_done", "gap_done", "th_done", "gates_done", "gatesT_ps",
                             "gatesT_done"))
        b2_done, b2_ps, acc_begun, gate_ps, gate_done = (
            sem(n) for n in ("b2_done", "b2_ps", "acc_begun", "gate_ps", "gate_done"))
        w1_split, w2_split = sem("w1_split"), sem("w2_split")
        up_ps, gelu_done, hi_dve, hi_act, h_split, down_ps, gated_done, acc_done = (
            sem(n) for n in ("up_ps", "gelu_done", "hi_dve", "hi_act", "h_split", "down_ps", "gated_done", "acc_done"))
        out_ps, out_done = sem("out_ps"), sem("out_done")

        tok = x.rearrange("b (p t) d -> p b t d", t=T)
        out_tok = out.rearrange("b (p t) d -> p b t d", t=T)
        w1_dram = W1.rearrange("e h i -> h e i")
        w2_dram = W2.rearrange("e (c p) d -> p e c d", p=P)

        wkT_bank = bank[3][:, 0:D]
        turned_bank = bank[5][:, 0:C_SMALL + R_ALL]
        ctxT_bank = bank[1][:, 0:B * M]
        bq33_bank = bank[6][:, 0:BIAS_ROWS]
        kT_bank = bank[2][:, 0:B * M]
        g_bank = bank[5][:, C_SMALL + R_ALL:C_SMALL + R_ALL + 2]
        bias_col_bank = [bank[5], bank[7]]
        v_bank = bank[0][:, 0:B * D].rearrange("p (b d) -> p b d", b=B)
        kq_bank = [bank[4], bank[7]]
        bias_row_bank = [bank[6], bank[6]]
        xT_bank = [bank[0], bank[1]]
        scores_bank = [bank[2], bank[3]]
        scoresT_bank = [bank[4], bank[5]]
        maxT_bank = [bank[5], bank[7]]
        half_bank = [bank[0], bank[1]]
        logits_bank = [bank[0], bank[1]]
        gatesT_bank = [bank[1], bank[0]]
        b2_bank = [bank[0], bank[1]]
        gate_bank = [bank[1], bank[0]]
        up_bank = [bank[4], bank[5], bank[6], bank[7]]
        down_bank = [bank[2], bank[3]]
        out0_bank = bank[1]
        out1_bank = [bank[0], bank[2]]

        HALVES = [slice(0, N // 2), slice(N // 2, N)]

        block = stack.enter_context(nc.Block())

        def part(start, size):
            return slice(start, start + size) if isinstance(start, int) else bass.ds(start, size)

        @block.sync
        def _(sp):
            sp.dma_start(wk_sb[:, :], Wk).then_inc(ld_wk, 16)
            sp.dma_start(x_sb[:, 0], tok[:, 0]).then_inc(ld_x[0], 16)
            sp.dma_start(qkv_rows[:, 1, :], bk.rearrange("(a d) -> a d", a=1)).then_inc(ld_bk, 16)
            sp.dma_start(wq_sb[:, :], Wq).then_inc(ld_wq, 16)
            sp.dma_start(qkv_rows[:, 0, :], bq.rearrange("(a d) -> a d", a=1)).then_inc(ld_bq, 16)
            sp.dma_start(x_sb[:, 1], tok[:, 1]).then_inc(ld_x[1], 16)
            sp.dma_start(wvo_sb[:, 0, :], Wv).then_inc(ld_wvo, 16)
            sp.dma_start(wvo_sb[:, 1, :], Wo).then_inc(ld_wvo, 16)
            sp.dma_start(smalls[R_WG:R_WG + E, :], Wg).then_inc(ld_small, 16)
            sp.dma_start(smalls[R_B1:R_B1 + E * C, :], b1.rearrange("e (c i) -> (e c) i", i=P)).then_inc(ld_small, 16)
            sp.dma_start(g_row[0:1, 0:1], g_xattn.rearrange("(a d) -> a d", a=1)).then_inc(ld_g, 16)
            sp.dma_start(g_row[0:1, 1:2], g_ffn.rearrange("(a d) -> a d", a=1)).then_inc(ld_g, 16)
            sp.dma_start(qkv_rows[:, 2, :], bv.rearrange("(a d) -> a d", a=1)).then_inc(ld_bv, 16)
            for e in range(E):
                sp.dma_start(raw1[:, e, :], W1[e]).then_inc(ld_w[e], 16)
                sp.dma_start(raw2[:, e, :].rearrange("p (c d) -> p c d", c=C),
                             W2[e].rearrange("(c p) d -> p c d", p=P)).then_inc(ld_w[e], 16)
            for r in (0, 32):
                sp.dma_start(b2_sb[r:r + E, :], b2).then_inc(ld_b2, 16)
            sp.wait_ge(out_done, 1)
            sp.dma_start(out_tok[:, 0], out_sb[:, 0]).then_inc(stored, 16)
            for half in range(2):
                tiles = slice(half * T // 2, (half + 1) * T // 2)
                sp.wait_ge(out_done, half + 2)
                sp.dma_start(out_tok[:, 1, tiles], out_sb[:, 1, tiles]).then_inc(stored, 16)
            sp.wait_ge(stored, 16 * 3)

        @block.gpsimd
        def _(pool):
            gp = nc.gpsimd
            gp.memset(ones[:, :], 1.0).then_inc(pool_step, 1)
            pool.wait_ge(pool_step, 1)
            gp.affine_select(out=ident[:, :], in_=ones[:, :], pattern=[[-1, P]], compare_op=ALU.is_equal, fill=0.0,
                             base=0, channel_multiplier=1).then_inc(ident_done, 1)
            gp.memset(sel33[:, :], 0.0).then_inc(pool_step, 1)
            gp.memset(head_mask[:, :], K_SCALE * HD ** -0.5).then_inc(pool_step, 1)
            gp.memset(neg_half[:, :], -0.5).then_inc(pool_step, 1)
            pool.wait_ge(pool_step, 4)
            for r in (0, 32):
                gp.memset(sel33[:, r:r + 1], 1.0).then_inc(sel33_done, 1)
            gp.affine_select(out=head_mask[:, :], in_=head_mask[:, :], pattern=[[-HD, H]], compare_op=ALU.is_ge,
                             fill=0.0, base=0, channel_multiplier=1).then_inc(pool_step, 1)
            pool.wait_ge(pool_step, 5)
            gp.affine_select(out=head_mask[:, :], in_=head_mask[:, :], pattern=[[HD, H]], compare_op=ALU.is_ge,
                             fill=0.0, base=HD - 1, channel_multiplier=-1).then_inc(head_mask_done, 1)
            gp.memset(ones33[:, :], 1.0).then_inc(ones33_done, 1)
            gp.memset(group_mask[:, :, :], 1.0).then_inc(pool_step, 1)
            gp.affine_select(out=ident_b[:, :], in_=ones[:, :], pattern=[[-1, P]], compare_op=ALU.is_equal, fill=0.0,
                             base=0, channel_multiplier=1).then_inc(max_consts, 1)
            gp.memset(max_hl[:, :, :, :], 0.0).then_inc(max_consts, 1)
            gp.memset(neg_sel[:, :, :, :], 0.0).then_inc(pool_step, 1)

            def rstd_of(n):
                pool.wait_ge(var_done, n + 1)
                gp.tensor_tensor(rstd[:, n % B, :], var_eps[:, n % B, :], neg_half[:, :],
                                 ALU.pow).then_inc(rstd_done, 1)

            rstd_of(0)
            pool.wait_ge(pool_step, 7)
            gp.affine_select(out=neg_sel[:, :, :, :], in_=neg_sel[:, :, :, :], pattern=[[-HG, G], [-1, HG], [0, M]],
                             compare_op=ALU.not_equal, fill=-1.0, base=0, channel_multiplier=1).then_inc(pool_step, 1)
            gp.affine_select(out=group_mask[:, :, :], in_=group_mask[:, :, :], pattern=[[0, G], [-M, HG]],
                             compare_op=ALU.is_ge, fill=0.0, base=0, channel_multiplier=1).then_inc(pool_step, 1)
            rstd_of(1)
            pool.wait_ge(pool_step, 9)
            gp.affine_select(out=neg_sel[:, :, :, :], in_=neg_sel[:, :, :, :], pattern=[[-HG, G], [-1, HG], [0, M]],
                             compare_op=ALU.not_equal, fill=-1.0, base=-32, channel_multiplier=1).then_inc(neg_sel_done, 1)
            gp.affine_select(out=group_mask[:, :, :], in_=group_mask[:, :, :], pattern=[[0, G], [M, HG]],
                             compare_op=ALU.is_ge, fill=0.0, base=M - 1, channel_multiplier=-1).then_inc(group_mask_done, 1)
            gp.memset(w_scale[:, :], W_SCALE).then_inc(pool_step, 1)
            gp.memset(unit[:, :], 1.0).then_inc(pool_step, 1)
            pool.wait_ge(pool_step, 11)

            def split_weights(e):
                pool.wait_ge(ld_w[e], 32)
                for n, (raw, hi, lo, done) in enumerate(((raw1, w1_hi, w1_lo, w1_split),
                                                         (raw2, w2_hi, w2_lo, w2_split))):
                    gp.tensor_tensor(raw[:, e, :], raw[:, e, :], w_scale[:, :], ALU.mult).then_inc(w_step, 1)
                    pool.wait_ge(w_step, 4 * e + 2 * n + 1)
                    gp.tensor_tensor(hi[:, e * I:(e + 1) * I], raw[:, e, :], unit[:, :], ALU.mult).then_inc(w_step, 1)
                    pool.wait_ge(w_step, 4 * e + 2 * n + 2)
                    gp.tensor_tensor(lo[:, e * I:(e + 1) * I], raw[:, e, :], hi[:, e * I:(e + 1) * I],
                                     ALU.subtract).then_inc(done, 1)

            for e in range(2):
                split_weights(e)
            gp.memset(pick_expert[:, :], 0.0).then_inc(pool_step, 1)
            gp.affine_select(out=ident_h[:, :], in_=ones[:, :], pattern=[[-1, P]], compare_op=ALU.is_equal, fill=0.0,
                             base=0, channel_multiplier=1).then_inc(gate_consts, 1)
            gp.memset(gates_hl[:, :, :, :], 0.0).then_inc(gate_consts, 1)
            gp.memset(b2_hi[:, :], 0.0).then_inc(gate_consts, 1)
            gp.memset(b2_lo[:, :], 0.0).then_inc(gate_consts, 1)
            gp.iota(expert_no[:, :, :], [[0, T], [1, E]], base=0, channel_multiplier=0,
                    allow_small_or_imprecise_dtypes=True).then_inc(gate_consts, 1)
            pool.wait_ge(pool_step, 12)
            gp.affine_select(out=pick_expert[:, :], in_=pick_expert[:, :], pattern=[[-1, E], [0, P]],
                             compare_op=ALU.not_equal, fill=1.0, base=0, channel_multiplier=1).then_inc(pool_step, 1)
            rstd_of(2)
            pool.wait_ge(pool_step, 13)
            gp.affine_select(out=pick_expert[:, :], in_=pick_expert[:, :], pattern=[[-1, E], [0, P]],
                             compare_op=ALU.not_equal, fill=1.0, base=-32, channel_multiplier=1).then_inc(gate_consts, 1)
            for e in range(2, E):
                split_weights(e)
            rstd_of(3)

            def add_step(b, s, k):
                pool.wait_ge(acc_done, s)
                pool.wait_ge(gated_done, s + 1)
                gp.tensor_tensor(accT[:, b, :], accT[:, b, :], gated[:, k, :], ALU.add).then_inc(acc_done, 1)

            for e in range(DVE_ADDS, E):
                add_step(0, e, e % 2)

            pool.wait_ge(acc_begun, B)
            with pool.Fori(0, E // 2 - 1) as pair:
                for k in range(2):
                    add_step(1, E + 2 * pair + k, k)
            add_step(1, S - 2, 0)

        @block.scalar
        def _(act):
            ac = nc.scalar
            act.dma_start(ctx_sb[:, :], ctx_in.rearrange("b m d -> (b m) d")).then_inc(ld_ctx, 16)

            def halves_high(dst, b, ready, done):
                for half, cols in enumerate(HALVES):
                    high_half(dst[:, b, cols], half_bank[half][:, 0:N // 2], ready, 2 * b + half + 1, done)

            def high_half(dst, src, ready, value, done):
                act.wait_ge(ready, value)
                ac.copy(dst, src).then_inc(done, 1)

            def x_high(b):
                high_half(x_hi[:, b, :], xT_bank[b][:, :], xT_ps, b + 1, x_hi_done)

            def kq_high(b):
                high_half(kq_hi[:, b, :], kq_bank[b][:, :], kq_ps, b + 1, kq_hi_done)

            def bias_high(b):
                high_half(bias33[:, b, :], bias_row_bank[b][0:BIAS_ROWS, :], bias_row_ps, b + 1, bias_hi_done)

            def bias_columns(b):
                act.wait_ge(bias_col_ps, b + 1)
                ac.activation(bias_col[:, b, :], bias_col_bank[b][:, 0:G], ACT.Copy, bias=P_LOG_SCALE,
                              scale=1.0 / K_SCALE).then_inc(bias_col_done, 1)

            def max_rows(b):
                act.wait_ge(maxT_ps, b + 1)
                ac.copy(maxT[:, b, :], maxT_bank[b][0:MAX_ROWS, 0:N // 2].bitcast(BF16)).then_inc(maxT_done, 1)

            def exponentials(b, g):
                act.wait_ge(scoresT_ps, b * G + g + 1)
                ac.activation(p32[:, b, g, :], scoresT_bank[g % 2][:, :], ACT.Exp, bias=bias_col[:, b, g:g + 1],
                              scale=1.0 / K_SCALE).then_inc(exp_done, 1)

            def p_high(b, g):
                act.wait_ge(exp_done, b * G + g + 1)
                ac.copy(p_hi[:, b, g, :], p32[:, b, g, :]).then_inc(p_hi_done, 1)

            def o_high(b):
                halves_high(o_hi, b, oT_ps, o_hi_done)

            def z_high(b):
                halves_high(z_hi, b, zT_ps, z_hi_done)

            def z_whole(b):
                act.wait_ge(z_lo_done, 2 * (b + 1))
                for half, cols in enumerate(HALVES):
                    ac.copy(zT[:, b, cols], half_bank[half][:, 0:N // 2]).then_inc(zT_done, 1)

            def router_tanh(b):
                act.wait_ge(gap_done, b + 1)
                ac.activation(th[:, b, :], gap[:, b, :], ACT.Tanh, scale=0.5).then_inc(th_done, 1)

            def gate_rows(b):
                act.wait_ge(gatesT_ps, b + 1)
                ac.copy(gatesT[:, b, :], gatesT_bank[b][0:GATE_ROWS, 0:N // 2].bitcast(F16)).then_inc(gatesT_done, 1)

            def begin_acc(b):
                act.wait_ge(b2_ps, b + 1)
                ac.activation(accT[:, b, :], b2_bank[b][:, :], ACT.Copy,
                              scale=1.0 / (GATE_SCALE * B2_SCALE)).then_inc(acc_begun, 1)

            def keep_gates(*experts):
                for e in experts:
                    act.wait_ge(gate_ps, e + 1)
                    ac.copy(gate_all[:, e, :], gate_bank[e % 2][:, :]).then_inc(gate_done, 1)

            def keep_gates1(s, k):
                act.wait_ge(gated_done, s - 1)
                act.wait_ge(gate_ps, s + 1)
                ac.copy(gate_now[:, k, :], gate_bank[1][:, :]).then_inc(gate_done, 1)

            def gelus(s, e, k, *chunks):
                if not isinstance(s, int) or s >= 2:
                    act.wait_ge(h_split, 2 * s - 2)
                for c in chunks or range(C):
                    act.wait_ge(up_ps, C * s + c + 1)
                    act.wait_ge(turned_done, 1)
                    ac.activation(h32[k][:, c, :], up_bank[c][:, :], ACT.Gelu, bias=smallT[:, part(R_B1 + e * C + c, 1)],
                                  scale=1.0 / W_SCALE).then_inc(gelu_done, 1)

            def hidden_high(s, k):
                if not isinstance(s, int) or s >= 2:
                    act.wait_ge(down_ps, s - 1)
                act.wait_ge(gelu_done, C * s + C)
                ac.activation(h_hi[:, k, 2:4, :], h32[k][:, 2:4, :], ACT.Copy, scale=H_SCALE).then_inc(hi_act, 1)

            act.wait_ge(wkT_ps, 1)
            ac.copy(wkT[:, :], wkT_bank).then_inc(wkT_done, 1)
            act.wait_ge(ctxT_ps, 1)
            ac.copy(ctxT[:, :], ctxT_bank).then_inc(ctxT_done, 1)
            act.wait_ge(bq33_ps, 1)
            ac.copy(bq33[:, :], bq33_bank).then_inc(bq33_done, 1)
            kq_high(0)
            x_high(0)
            bias_high(0)
            act.wait_ge(turned_ps, 1)
            ac.copy(turned[:, :], turned_bank).then_inc(turned_done, 1)
            act.wait_ge(g_ps, 1)
            ac.activation(tanh_g[:, :], g_bank, ACT.Tanh).then_inc(tanh_done, 1)
            bias_columns(0)
            kq_high(1)
            max_rows(0)
            bias_high(1)
            x_high(1)
            act.wait_ge(bias_col_done, 1)
            for g in range(G):
                exponentials(0, g)
                p_high(0, g)
            bias_columns(1)
            max_rows(1)
            o_high(0)
            act.wait_ge(bias_col_done, 2)
            for g in range(G):
                exponentials(1, g)
                if g < 2:
                    p_high(1, g)
            ac.activation(gelu_first[:, :], ones[:, 0:1], ACT.Gelu)
            z_high(0)
            z_whole(0)
            p_high(1, 2)
            gelus(0, 0, 0)
            hidden_high(0, 0)
            p_high(1, 3)
            gelus(1, 1, 1)
            hidden_high(1, 1)
            router_tanh(0)
            gelus(2, 2, 0)
            hidden_high(2, 0)
            gate_rows(0)
            begin_acc(0)
            keep_gates(0, 1)
            gelus(3, 3, 1)
            hidden_high(3, 1)
            keep_gates(2, 3)
            gelus(4, 4, 0, 0, 1)
            keep_gates(4)
            gelus(4, 4, 0, 2, 3)
            keep_gates(5)
            hidden_high(4, 0)
            keep_gates(6, 7)
            gelus(5, 5, 1)
            o_high(1)
            hidden_high(5, 1)
            gelus(6, 6, 0)
            hidden_high(6, 0)
            gelus(7, 7, 1, 0, 1)
            z_high(1)
            gelus(7, 7, 1, 2, 3)
            z_whole(1)
            hidden_high(7, 1)
            gelus(E, 0, 0)
            router_tanh(1)
            hidden_high(E, 0)
            gelus(E + 1, 1, 1)
            hidden_high(E + 1, 1)
            gate_rows(1)
            begin_acc(1)
            keep_gates1(E, 0)
            with act.Fori(0, E // 2 - 1) as pair:
                for k in range(2):
                    s, e = E + 2 * pair + k, 2 * pair + k
                    gelus(s + 2, e + 2, k)
                    hidden_high(s + 2, k)
                    keep_gates1(s + 1, 1 - k)
            keep_gates1(S - 1, 1)

        @block.tensor
        def _(pe):
            te = nc.tensor

            def product(out_, a_hi, a_lo, b_hi, b_lo, start=True, stop=True):
                te.matmul(out_, a_hi, b_hi, start=start, stop=False, skip_group_check=True)
                te.matmul(out_, a_hi, b_lo, start=False, stop=False, skip_group_check=True)
                return te.matmul(out_, a_lo, b_hi, start=False, stop=stop, skip_group_check=True)

            def transpose_x(b):
                pe.wait_ge(xln_done, 2 * (b + 1))
                for t in range(T):
                    t_ = te.transpose(xT_bank[b][:, t * P:(t + 1) * P], xln[:, b, t, :], ident[:, :])
                t_.then_inc(xT_ps, 1)

            def keys(b):
                pe.wait_ge(kbd_done, b + 1)
                te.matmul(kq_bank[b][:, :], wq_sb[:, :], k_bd[:, b].rearrange("p h m -> p (h m)"), start=True,
                          stop=True).then_inc(kq_ps, 1)

            def bias_row(b):
                te.matmul(bias_row_bank[b][0:BIAS_ROWS, :], bq33[:, :], k_bd[:, b].rearrange("p h m -> p (h m)"),
                          start=True, stop=True).then_inc(bias_row_ps, 1)

            def scores(b, *tiles):
                for t in tiles:
                    if t == 0:
                        pe.wait_ge(x_hi_done, b + 1)
                        pe.wait_ge(x_lo_done, b + 1)
                        pe.wait_ge(kq_hi_done, b + 1)
                        pe.wait_ge(kq_lo_done, b + 1)
                    n = b * T + t
                    if n >= 2:
                        pe.wait_ge(max_done, n - 1)
                    rows = slice(t * P, (t + 1) * P)
                    product(scores_bank[n % 2][:, :], x_hi[:, b, rows], x_lo[:, b, rows], kq_hi[:, b, :],
                            kq_lo[:, b, :], stop=False)
                    if t == 0:
                        pe.wait_ge(bias_lo_done, b + 1)
                    te.matmul(scores_bank[n % 2][:, :], ones33[:, :], bias33[:, b, :], start=False, stop=True,
                              skip_group_check=True).then_inc(scores_ps, 1)

            def bias_columns(b):
                pe.wait_ge(bias_lo_done, b + 1)
                for g in range(G):
                    t_ = te.matmul(bias_col_bank[b][:, g:g + 1], bias33[:, b, g * P:(g + 1) * P], ones33[:, 0:1],
                                   start=True, stop=True)
                t_.then_inc(bias_col_ps, 1)

            def transpose_max(b):
                pe.wait_ge(max_split, b + 1)
                pe.wait_ge(bias_col_done, b + 1)
                for t in range(T):
                    t_ = te.transpose(maxT_bank[b][0:MAX_ROWS, t * P // 2:(t + 1) * P // 2].bitcast(BF16),
                                      max_hl[:, b, t, :], ident_b[:, :])
                t_.then_inc(maxT_ps, 1)

            def scores_transposed(b, *groups):
                for g in groups:
                    n = b * G + g
                    if g == 0:
                        pe.wait_ge(maxT_done, b + 1)
                        pe.wait_ge(neg_sel_done, 1)
                    if n >= 2:
                        pe.wait_ge(exp_done, n - 1)
                    rows = slice(g * P, (g + 1) * P)
                    product(scoresT_bank[n % 2][:, :], kq_hi[:, b, rows], kq_lo[:, b, rows], x_hi[:, b, :],
                            x_lo[:, b, :], stop=False)
                    te.matmul(scoresT_bank[n % 2][:, :], neg_sel[:, g].rearrange("p h m -> p (h m)"), maxT[:, b, :],
                              start=False, stop=True, skip_group_check=True).then_inc(scoresT_ps, 1)

            def values(b):
                pe.wait_ge(p_hi_done, (b + 1) * G)
                pe.wait_ge(p_lo_done, (b + 1) * G)
                for half in range(2):
                    for u in range(2):
                        t = 2 * half + u
                        rows = slice(t * P, (t + 1) * P)
                        for g in range(G):
                            at = (u * G + g) * VC
                            first = u == 0 and g == 0
                            last = u == 1 and g == G - 1
                            full = half_bank[half][:, at:at + VC]
                            te.matmul(full, p_hi[:, b, g, rows], vr[:, b, g, :], start=first, stop=False,
                                      skip_group_check=True)
                            te.matmul(full[:, 0:HG * HD], p_hi[:, b, g, rows], v_lo[:, b, g, :], start=False,
                                      stop=False, skip_group_check=True)
                            t_ = te.matmul(full, p_lo[:, b, g, rows], vr[:, b, g, :], start=False, stop=last,
                                           skip_group_check=True)
                    t_.then_inc(pv_ps, 1)

            def transpose_halves(b, src, ready, done):
                for half in range(2):
                    pe.wait_ge(ready, 2 * b + half + 1)
                    for u in range(2):
                        t_ = te.transpose(half_bank[half][:, u * P:(u + 1) * P], src[:, b, 2 * half + u, :],
                                          ident[:, :])
                    t_.then_inc(done, 1)

            def attention_out(b):
                for half in range(2):
                    pe.wait_ge(o_hi_done, 2 * b + half + 1)
                    pe.wait_ge(o_lo_done, 2 * b + half + 1)
                    for u in range(2):
                        rows = slice((2 * half + u) * P, (2 * half + u + 1) * P)
                        t_ = product(half_bank[half][:, u * P:(u + 1) * P], o_hi[:, b, rows], o_lo[:, b, rows],
                                     wo_hi[:, :], wo_lo[:, :], start=(u == 0), stop=(u == 1))
                    t_.then_inc(attn_ps, 1)

            def router(b):
                pe.wait_ge(zT_done, 2 * (b + 1))
                for t in range(T):
                    t_ = te.matmul(logits_bank[b][:, t * E:(t + 1) * E], zT[:, b, t * P:(t + 1) * P],
                                   smallT[:, R_WG:R_WG + E], start=True, stop=True)
                t_.then_inc(logits_ps, 1)

            def transpose_gates(b):
                pe.wait_ge(gates_done, b + 1)
                pe.wait_ge(z_lo_done, 2 * (b + 1))
                for t in range(T):
                    t_ = te.transpose(gatesT_bank[b][0:GATE_ROWS, t * P // 2:(t + 1) * P // 2].bitcast(F16),
                                      gates_hl[:, b, t, :], ident_h[:, :])
                t_.then_inc(gatesT_ps, 1)

            def b2_sum(b):
                pe.wait_ge(gatesT_done, b + 1)
                te.matmul(b2_bank[b][:, :], b2_hi[:, :], gatesT[:, b, :], start=True, stop=False)
                te.matmul(b2_bank[b][:, :], b2_lo[:, :], gatesT[:, b, :], start=False, stop=True).then_inc(b2_ps, 1)

            def spread_gates0(*experts):
                for e in experts:
                    if e == 1:
                        pe.wait_ge(acc_begun, 1)
                    elif e > 1:
                        pe.wait_ge(gate_done, e - 1)
                    te.matmul(gate_bank[e % 2][:, :], pick_expert[:, e * P:(e + 1) * P], gatesT[:, 0, :], start=True,
                              stop=True).then_inc(gate_ps, 1)

            def spread_gates1(s, e):
                pe.wait_ge(gate_done, s)
                te.matmul(gate_bank[1][:, :], pick_expert[:, part(e * P, P)], gatesT[:, 1, :], start=True,
                          stop=True).then_inc(gate_ps, 1)

            def up(s, b, e, *chunks):
                for c in chunks or range(C):
                    if not isinstance(s, int) or s >= 1:
                        pe.wait_ge(gelu_done, C * s - C + c + 1)
                    cols = part(e * I + c * P, P)
                    product(up_bank[c][:, :], w1_hi[:, cols], w1_lo[:, cols], z_hi[:, b, :],
                            z_lo[:, b, :]).then_inc(up_ps, 1)

            def down(s, e, k):
                if not isinstance(s, int) or s >= 2:
                    pe.wait_ge(gated_done, s - 1)
                for c in range(C):
                    if c % 2 == 0:
                        pe.wait_ge(h_split, 2 * s + c // 2 + 1)
                    cols = part(e * C * D + c * D, D)
                    t_ = product(down_bank[k][:, :], w2_hi[:, cols], w2_lo[:, cols], h_hi[:, k, c, :], h_lo[:, k, c, :],
                                 start=(c == 0), stop=(c == C - 1))
                t_.then_inc(down_ps, 1)

            def up0(e, *chunks):
                pe.wait_ge(w1_split, e + 1)
                up(e, 0, e, *chunks)

            def down0(e):
                pe.wait_ge(w2_split, e + 1)
                down(e, e, e % 2)

            def transpose_out0():
                pe.wait_ge(acc_done, E)
                pe.wait_ge(acc_begun, B)
                for t in range(T):
                    rows = slice(t * P, (t + 1) * P)
                    t_ = te.transpose(out0_bank[:, rows], accT[:, 0, rows], ident[:, :])
                t_.then_inc(out_ps, 1)

            def turn_back(src, start, stop):
                for half in range(2):
                    if stop:
                        pe.wait_ge(gated_done, S + half)
                    for u in range(2):
                        rows = slice((2 * half + u) * P, (2 * half + u + 1) * P)
                        t_ = te.matmul(out1_bank[half][:, u * P:(u + 1) * P], src[:, rows], ident[:, :],
                                       start=(start and u == 0), stop=(stop and u == 1), skip_group_check=True)
                    if stop:
                        t_.then_inc(out_ps, 1)

            pe.wait_ge(ident_done, 1)
            pe.wait_ge(ld_wk, 16)
            te.transpose(wkT_bank, wk_sb[:, :], ident[:, :]).then_inc(wkT_ps, 1)
            pe.wait_ge(ld_ctx, 16)
            te.transpose(ctxT_bank, ctx_sb[:, :], ident[0:B * M, 0:B * M]).then_inc(ctxT_ps, 1)
            pe.wait_ge(wkT_done, 1)
            pe.wait_ge(ctxT_done, 1)
            te.matmul(kT_bank, wkT[:, :], ctxT[:, :], start=True, stop=False)
            pe.wait_ge(ld_bk, 16)
            te.matmul(kT_bank, qkv_rows[:, 1, :], ones[0:1, 0:B * M], start=False, stop=True).then_inc(kT_ps, 1)
            pe.wait_ge(sel33_done, 2)
            pe.wait_ge(ld_bq, 16)
            te.matmul(bq33_bank, qkv_rows[:, 0, :], sel33[:, :], start=True, stop=True).then_inc(bq33_ps, 1)
            pe.wait_ge(ld_wq, 16)
            keys(0)
            transpose_x(0)
            pe.wait_ge(bq33_done, 1)
            bias_row(0)
            pe.wait_ge(ld_wvo, 32)
            for w in range(2):
                te.transpose(turned_bank[:, w * D:(w + 1) * D], wvo_sb[:, w, :], ident[:, :])
            pe.wait_ge(ld_small, 32)
            te.transpose(turned_bank[:, C_SMALL:C_SMALL + R_ALL], smalls[:, :],
                         ident[0:R_ALL, 0:R_ALL]).then_inc(turned_ps, 1)
            pe.wait_ge(kbd_done, 2)
            pe.wait_ge(ones33_done, 1)
            scores(0, 0, 1)
            pe.wait_ge(ld_g, 32)
            pe.wait_ge(turned_done, 1)
            te.matmul(g_bank, ones[0:1, :], g_row[:, :], start=True, stop=True).then_inc(g_ps, 1)
            scores(0, 2, 3)
            pe.wait_ge(tanh_done, 1)
            bias_columns(0)
            keys(1)
            pe.wait_ge(bias_lo_done, 1)
            bias_row(1)
            pe.wait_ge(max_consts, 2)
            transpose_max(0)
            transpose_x(1)
            pe.wait_ge(ctxT4_done, 1)
            pe.wait_ge(ld_bv, 16)
            for b in range(B):
                te.matmul(v_bank[:, b, :], ctxT4[:, b].rearrange("p h m -> p (h m)"), wvT, start=True, stop=False)
                t_ = te.matmul(v_bank[:, b, :], ones[0:1, :], qkv_rows[:, 2, :], start=False, stop=True)
            t_.then_inc(v_ps, 1)
            for g in range(G):
                scores_transposed(0, g)
                scores(1, g)
            bias_columns(1)
            pe.wait_ge(v_done, 1)
            values(0)
            transpose_max(1)
            transpose_halves(0, o32, o_done, oT_ps)
            scores_transposed(1, 0)
            pe.wait_ge(wo_done, 1)
            attention_out(0)
            scores_transposed(1, 1, 2, 3)
            transpose_halves(0, zln, zln_done, zT_ps)
            pe.wait_ge(z_hi_done, 2)
            pe.wait_ge(z_lo_done, 2)
            pe.wait_ge(exp_done, B * G)
            up0(0)
            router(0)
            up0(1)
            down0(0)
            up0(2)
            down0(1)
            pe.wait_ge(gate_consts, 6)
            transpose_gates(0)
            up0(3, 0, 1)
            b2_sum(0)
            spread_gates0(0)
            up0(3, 2, 3)
            spread_gates0(1)
            down0(2)
            spread_gates0(2, 3)
            up0(4, 0, 1)
            spread_gates0(4)
            up0(4, 2, 3)
            spread_gates0(5)
            down0(3)
            spread_gates0(6, 7)
            up0(5, 0, 1)
            pe.wait_ge(gate_done, E)
            values(1)
            up0(5, 2, 3)
            transpose_halves(1, o32, o_done, oT_ps)
            down0(4)
            attention_out(1)
            up0(6)
            down0(5)
            up0(7, 0, 1)
            transpose_halves(1, zln, zln_done, zT_ps)
            up0(7, 2, 3)
            down0(6)
            router(1)
            pe.wait_ge(z_hi_done, 4)
            pe.wait_ge(z_lo_done, 4)
            up(E, 1, 0)
            down0(7)
            up(E + 1, 1, 1)
            transpose_gates(1)
            down(E, 0, 0)
            b2_sum(1)
            spread_gates1(E, 0)
            with pe.Fori(0, E // 2 - 1) as pair:
                for k in range(2):
                    s, e = E + 2 * pair + k, 2 * pair + k
                    up(s + 2, 1, e + 2)
                    spread_gates1(s + 1, e + 1)
                    down(s + 1, e + 1, 1 - k)
            spread_gates1(S - 1, E - 1)
            transpose_out0()
            down(S - 1, E - 1, 1)
            pe.wait_ge(acc_done, S - 1)
            pe.wait_ge(gate_done, S)
            turn_back(accT[:, 1, :], True, False)
            turn_back(gated[:, 1, :], False, True)

        @block.vector
        def _(dve):
            ve = nc.vector
            count = [0]

            def link(ins):
                count[0] += 1
                ins.then_inc(dve_step, 1)
                dve.wait_ge(dve_step, count[0])

            def stats_of(src, b, *tiles):
                for t in tiles:
                    i_ = ve.bn_stats(stats[:, b, t, :], src[:, b, t, :])
                return i_

            def moments_of(b, last_stats):
                link(last_stats)
                for t in range(T):
                    i_ = ve.bn_aggr(moments[:, b, t, :], stats[:, b, t, :])
                link(i_)
                ve.tensor_scalar(var_eps[:, b, :], moments[:, b, :, 1], LN_EPS, None, ALU.add).then_inc(var_done, 1)

            def normalise(dst, src, b, value, done):
                dve.wait_ge(rstd_done, value)
                for t in range(T):
                    i_ = ve.tensor_scalar(dst[:, b, t, :], src[:, b, t, :], moments[:, b, t, 0:1],
                                          rstd[:, b, t:t + 1], ALU.subtract, ALU.mult)
                    if t % 2 == 1:
                        i_.then_inc(done, 1)

            def apart(b):
                ve.tensor_tensor(k_bd[:, b], kT_bank[:, b * M:(b + 1) * M].unsqueeze(1).to_broadcast([P, H, M]),
                                 head_mask[:, :].unsqueeze(2).to_broadcast([P, H, M]), ALU.mult).then_inc(kbd_done, 1)

            def low_half(dst, src, high, done, value):
                dve.wait_ge(done, value)
                return ve.tensor_tensor(dst, src, high, ALU.subtract)

            def x_low(b):
                low_half(x_lo[:, b, :], xT_bank[b][:, :], x_hi[:, b, :], x_hi_done, b + 1).then_inc(x_lo_done, 1)

            def keys_low(b):
                low_half(kq_lo[:, b, :], kq_bank[b][:, :], kq_hi[:, b, :], kq_hi_done, b + 1).then_inc(kq_lo_done, 1)

            def bias_low(b):
                low_half(bias33[32:33, b, :], bias_row_bank[b][32:33, :], bias33[32:33, b, :], bias_hi_done,
                         b + 1).then_inc(bias_lo_done, 1)

            def maxima(b, *tiles):
                for t in tiles:
                    n = b * T + t
                    dve.wait_ge(scores_ps, n + 1)
                    ve.tensor_reduce(maxes[:, b, t, :], scores_bank[n % 2][:, :].rearrange("p (h m) -> p h m", h=H),
                                     AX.X, ALU.max).then_inc(max_done, 1)

            def split_maxima(b):
                dve.wait_ge(max_done, T * (b + 1))
                link(ve.tensor_copy(max_hl[:, b, :, 0:H], maxes[:, b, :, :]))
                ve.tensor_tensor(max_hl[:, b, :, 32:32 + H], maxes[:, b, :, :], max_hl[:, b, :, 0:H],
                                 ALU.subtract).then_inc(max_split, 1)

            def values():
                dve.wait_ge(v_ps, 1)
                for b in range(B):
                    link(ve.tensor_tensor(
                        v32[:, b, :].rearrange("p (g h d) -> p (g h) d", g=G, h=HG),
                        v_bank[:, b, :].rearrange("p (g h d) -> p (g h) d", g=G, h=HG),
                        group_mask[:, :, :].rearrange("p g h -> p (g h)").unsqueeze(2).to_broadcast([P, H, HD]),
                        ALU.mult))
                    v_ = v32[:, b, :].rearrange("p (g c) -> p g c", g=G)
                    ve.tensor_scalar(vr[:, b, :, HG * HD:VC], group_mask[:, :, :], 1.0 / O_SCALE, None, ALU.mult)
                    link(ve.tensor_copy(vr[:, b, :, 0:HG * HD], v_))
                    i_ = ve.tensor_tensor(v_lo[:, b, :, :], v_, vr[:, b, :, 0:HG * HD], ALU.subtract)
                i_.then_inc(v_done, 1)

            def output_weights():
                dve.wait_ge(tanh_done, 1)
                dve.wait_ge(turned_done, 1)
                link(ve.tensor_scalar(wo32[:, :], woT, tanh_g[:, 0:1], WO_SCALE, ALU.mult, ALU.mult))
                link(ve.tensor_copy(wo_hi[:, :], wo32[:, :]))
                ve.tensor_tensor(wo_lo[:, :], wo32[:, :], wo_hi[:, :], ALU.subtract).then_inc(wo_done, 1)

            def router_constants():
                ve.tensor_scalar(half_gate[:, 0:1], tanh_g[:, 1:2], 0.5 * GATE_SCALE, None, ALU.mult)
                ve.tensor_scalar(half_gate[:, 1:2], tanh_g[:, 1:2], -0.5 * GATE_SCALE, None, ALU.mult)
                dve.wait_ge(ld_b2, 32)
                for r in (0, 32):
                    rows = slice(r, r + E)
                    i_ = ve.tensor_scalar(b2_hi[rows, :], b2_sb[rows, :], B2_SCALE, None, ALU.mult)
                link(i_)
                for r in (0, 32):
                    rows = slice(r, r + E)
                    i_ = ve.scalar_tensor_tensor(out=b2_lo[rows, :], in0=b2_sb[rows, :], scalar=B2_SCALE,
                                                 in1=b2_hi[rows, :], op0=ALU.mult, op1=ALU.subtract)
                i_.then_inc(b2_done, 1)

            def p_low(b, g):
                dve.wait_ge(p_hi_done, b * G + g + 1)
                ve.tensor_tensor(p_lo[:, b, g, :], p32[:, b, g, :], p_hi[:, b, g, :],
                                 ALU.subtract).then_inc(p_lo_done, 1)

            def normalise_heads(b, half):
                dve.wait_ge(pv_ps, 2 * b + half + 1)
                sums = half_bank[half][:, 0:2 * G * VC].rearrange("p (u c) -> p u c", c=VC)
                r_ = r_den[:, b, 2 * half:2 * half + 2].rearrange("p t g h -> p (t g) h")
                link(ve.reciprocal(r_, sums[:, :, HG * HD:VC]))
                ve.tensor_tensor(
                    o32[:, b, 2 * half:2 * half + 2, :].rearrange("p t (g h d) -> p (t g) h d", g=G, h=HG),
                    sums[:, :, 0:HG * HD].rearrange("p u (h d) -> p u h d", h=HG),
                    r_.unsqueeze(3).to_broadcast([P, 2 * G, HG, HD]), ALU.mult).then_inc(o_done, 1)

            def halves_low(dst, high, b, high_done, done):
                for half, cols in enumerate(HALVES):
                    low_half(dst[:, b, cols], half_bank[half][:, 0:N // 2], high[:, b, cols], high_done,
                             2 * b + half + 1).then_inc(done, 1)

            def o_low(b):
                halves_low(o_lo, o_hi, b, o_hi_done, o_lo_done)

            def residual(b):
                for half in range(2):
                    tiles = slice(2 * half, 2 * half + 2)
                    dve.wait_ge(attn_ps, 2 * b + half + 1)
                    link(ve.scalar_tensor_tensor(
                        out=x1[:, b, tiles].rearrange("p t d -> p (t d)"), in0=half_bank[half][:, 0:N // 2],
                        scalar=1.0 / (O_SCALE * WO_SCALE), in1=x_sb[:, b, tiles].rearrange("p t d -> p (t d)"),
                        op0=ALU.mult, op1=ALU.add))
                    i_ = stats_of(x1, b, 2 * half, 2 * half + 1)
                moments_of(b, i_)

            def z_low(b):
                halves_low(z_lo, z_hi, b, z_hi_done, z_lo_done)

            def wide(ap):
                return ap.unsqueeze(2).to_broadcast([P, T, E])

            def first_of(b, values_, top, pick):
                link(ve.tensor_reduce(top[:, b, :], values_, AX.X, ALU.max))
                link(ve.tensor_tensor(r_a[:, b], values_, wide(top[:, b, :]), ALU.is_equal))
                link(ve.scalar_tensor_tensor(out=r_b[:, b], in0=r_a[:, b], scalar=-float(E), in1=expert_no[:, :, :],
                                             op0=ALU.mult, op1=ALU.add))
                link(ve.tensor_reduce(least[:, b, :], r_b[:, b], AX.X, ALU.min))
                link(ve.tensor_tensor(pick[:, b], r_b[:, b], wide(least[:, b, :]), ALU.is_equal))

            def choose(b):
                dve.wait_ge(logits_ps, b + 1)
                ve.tensor_copy(logits[:, b].rearrange("p t e -> p (t e)"),
                               logits_bank[b][:, 0:T * E]).then_inc(logits_done, 1)
                dve.wait_ge(logits_done, b + 1)
                first_of(b, logits[:, b], top1, pick1)
                link(ve.scalar_tensor_tensor(out=logits[:, b], in0=pick1[:, b], scalar=MASKED, in1=logits[:, b],
                                             op0=ALU.mult, op1=ALU.add))
                first_of(b, logits[:, b], top2, pick2)
                ve.tensor_tensor(gap[:, b, :], top1[:, b, :], top2[:, b, :], ALU.subtract).then_inc(gap_done, 1)

            def weigh(b):
                dve.wait_ge(th_done, b + 1)
                ve.tensor_scalar(w_1[:, b, :], th[:, b, :], 1.0, half_gate[:, 0:1], ALU.add, ALU.mult)
                link(ve.tensor_scalar(w_2[:, b, :], th[:, b, :], -1.0, half_gate[:, 1:2], ALU.add, ALU.mult))
                ve.tensor_tensor(pick1[:, b], pick1[:, b], wide(w_1[:, b, :]), ALU.mult)
                link(ve.tensor_tensor(pick2[:, b], pick2[:, b], wide(w_2[:, b, :]), ALU.mult))
                link(ve.tensor_tensor(gates[:, b], pick1[:, b], pick2[:, b], ALU.add))
                link(ve.tensor_copy(gates_hl[:, b, :, 0:E], gates[:, b]))
                ve.tensor_tensor(gates_hl[:, b, :, 32:32 + E], gates[:, b], gates_hl[:, b, :, 0:E],
                                 ALU.subtract).then_inc(gates_done, 1)

            def split_hidden(s, k, *halves):
                if not isinstance(s, int) or s >= 2:
                    dve.wait_ge(down_ps, s - 1)
                for j in halves or range(2):
                    chunks = slice(2 * j, 2 * j + 2)
                    if j == 0:
                        dve.wait_ge(gelu_done, C * s + 2)
                        ve.tensor_scalar(h_hi[:, k, chunks, :], h32[k][:, chunks, :], H_SCALE, None,
                                         ALU.mult).then_inc(hi_dve, 1)
                        dve.wait_ge(hi_dve, s + 1)
                    else:
                        dve.wait_ge(hi_act, s + 1)
                    ve.scalar_tensor_tensor(out=h_lo[:, k, chunks, :], in0=h32[k][:, chunks, :], scalar=H_SCALE,
                                            in1=h_hi[:, k, chunks, :], op0=ALU.mult,
                                            op1=ALU.subtract).then_inc(h_split, 1)

            def gate(s, b, e, k, columns=slice(0, N)):
                dve.wait_ge(gate_done, s + 1)
                if not isinstance(s, int) or s >= 2:
                    dve.wait_ge(acc_done, s - 1)
                dve.wait_ge(down_ps, s + 1)
                gates_ = gate_now[:, k, columns] if b else gate_all[:, e, columns]
                ve.scalar_tensor_tensor(out=gated[:, k, columns], in0=down_bank[k][:, columns],
                                        scalar=1.0 / (H_SCALE * W_SCALE * GATE_SCALE), in1=gates_, op0=ALU.mult,
                                        op1=ALU.mult).then_inc(gated_done, 1)

            def accumulate0(e):
                gate(e, 0, e, e % 2)
                dve.wait_ge(acc_begun, 1)
                if e >= 1:
                    dve.wait_ge(acc_done, e)
                dve.wait_ge(gated_done, e + 1)
                ve.tensor_tensor(accT[:, 0, :], accT[:, 0, :], gated[:, e % 2, :], ALU.add).then_inc(acc_done, 1)

            def finish(b, tiles, rows, value):
                dve.wait_ge(out_ps, value)
                ve.tensor_tensor(out_sb[:, b, tiles, :].rearrange("p t d -> p (t d)"), rows,
                                 x1[:, b, tiles, :].rearrange("p t d -> p (t d)"), ALU.add).then_inc(out_done, 1)

            dve.wait_ge(ld_x[0], 16)
            moments_of(0, stats_of(x_sb, 0, *range(T)))
            dve.wait_ge(kT_ps, 1)
            dve.wait_ge(head_mask_done, 1)
            apart(0)
            normalise(xln, x_sb, 0, 1, xln_done)
            apart(1)
            keys_low(0)
            x_low(0)
            bias_low(0)
            dve.wait_ge(ld_x[1], 16)
            maxima(0, 0, 1)
            moments_of(1, stats_of(x_sb, 1, *range(T)))
            maxima(0, 2, 3)
            dve.wait_ge(max_consts, 2)
            split_maxima(0)
            dve.wait_ge(ctxT_done, 1)
            ve.tensor_copy(ctxT4[:, :, :, :], ctxT[:, :].rearrange("p (b m) -> p b m", b=B).unsqueeze(2).to_broadcast(
                [P, B, HG, M])).then_inc(ctxT4_done, 1)
            normalise(xln, x_sb, 1, 2, xln_done)
            keys_low(1)
            bias_low(1)
            x_low(1)
            dve.wait_ge(group_mask_done, 1)
            values()
            for g in range(G):
                p_low(0, g)
                maxima(1, g)
            split_maxima(1)
            normalise_heads(0, 0)
            normalise_heads(0, 1)
            output_weights()
            o_low(0)
            residual(0)
            p_low(1, 0)
            p_low(1, 1)
            normalise(zln, x1, 0, B + 1, zln_done)
            z_low(0)
            dve.wait_ge(gate_consts, 6)
            router_constants()
            split_hidden(0, 0)
            choose(0)
            split_hidden(1, 1)
            weigh(0)
            split_hidden(2, 0)
            accumulate0(0)
            split_hidden(3, 1)
            accumulate0(1)
            p_low(1, 2)
            p_low(1, 3)
            split_hidden(4, 0)
            accumulate0(2)
            normalise_heads(1, 0)
            normalise_heads(1, 1)
            split_hidden(5, 1, 0)
            o_low(1)
            split_hidden(5, 1, 1)
            gate(3, 0, 3, 1)
            residual(1)
            split_hidden(6, 0, 0)
            normalise(zln, x1, 1, B + 2, zln_done)
            split_hidden(6, 0, 1)
            gate(4, 0, 4, 0)
            split_hidden(7, 1, 0)
            z_low(1)
            split_hidden(7, 1, 1)
            gate(5, 0, 5, 1)
            choose(1)
            gate(6, 0, 6, 0)
            split_hidden(E, 0, 0)
            weigh(1)
            split_hidden(E, 0, 1)
            gate(7, 0, 7, 1)
            with dve.Fori(0, E // 2 - 1) as pair:
                for k in range(2):
                    s, e = E + 2 * pair + k, 2 * pair + k
                    split_hidden(s + 1, 1 - k)
                    gate(s, 1, e, k)
            split_hidden(S - 1, 1, 0)
            gate(S - 2, 1, E - 2, 0)
            split_hidden(S - 1, 1, 1)
            finish(0, slice(0, T), out0_bank[:, :], 1)
            for half in range(2):
                gate(S - 1, 1, E - 1, 1, HALVES[half])
            for half in range(2):
                finish(1, slice(2 * half, 2 * half + 2), out1_bank[half][:, 0:N // 2], 2 + half)


INS = ["x", "ctx_1024", "g_xattn", "g_ffn", "L0_xattn_Wq", "L0_xattn_bq", "L0_xattn_Wk", "L0_xattn_bk", "L0_xattn_Wv",
       "L0_xattn_bv", "L0_xattn_Wo", "L0_ffn_Wg", "L0_ffn_W1", "L0_ffn_b1", "L0_ffn_W2", "L0_ffn_b2"]


def kernel(**inputs):
    import numpy as np
    import concourse.bacc as bacc
    from concourse.bass_utils import run_bass_kernel_spmd

    nc = bacc.Bacc("TRN2", target_bir_lowering=False, num_devices=1)
    arrays, args = {}, []
    for name in INS:
        a = np.ascontiguousarray(inputs[name])
        arrays[name] = a
        args.append(nc.dram_tensor(name, a.shape, mybir.dt.from_np(a.dtype), kind="ExternalInput").ap())
    out = nc.dram_tensor("out", arrays["x"].shape, F32, kind="ExternalOutput").ap()
    gated_block(nc, *args, out)
    r = run_bass_kernel_spmd(nc, [arrays], core_ids=[0])
    return r.results[0]["out"]
```

```python
from contextlib import ExitStack

import concourse.bass as bass
from concourse import mybir

ALU = mybir.AluOpType
ACT = mybir.ActivationFunctionType
AX = mybir.AxisListType
F32 = mybir.dt.float32
F16 = mybir.dt.float16
BF16 = mybir.dt.bfloat16

LN_EPS = 1e-5
K_SCALE = 16.0
P_LOG_SCALE = 5.545177444479562
GATE_SCALE = 16.0
B2_SCALE = 16.0
O_SCALE = 16.0
WO_SCALE = 16.0
W_SCALE = 256.0
H_SCALE = 16.0
MASKED = -3.0e38


def gated_block(nc, x, ctx_in, g_xattn, g_ffn, Wq, bq, Wk, bk, Wv, bv, Wo, Wg, W1, b1, W2, b2, out):
    B, N, D = x.shape
    M = ctx_in.shape[1]
    H = 16
    HD = D // H
    E, _, I = W1.shape
    P = 128
    T = N // P
    G = H * M // P
    HG = H // G
    C = I // P
    VC = HG * HD + HG
    BIAS_ROWS = 33
    MAX_ROWS = 32 + H
    GATE_ROWS = 32 + E
    assert (B, N, D, M, E, I) == (2, 512, 128, 32, 8, 512)
    R_WG, R_B1, R_ALL = 0, E, E + E * C
    C_SMALL = 2 * D
    DVE_ADDS = 3
    S = B * E

    with ExitStack() as stack:
        def sb(name, shape, dt):
            return stack.enter_context(nc.sbuf_tensor(name, shape, dt))

        def sem(name):
            return stack.enter_context(nc.semaphore(name))

        bank = [stack.enter_context(nc.psum_tensor(f"bank{i}", [P, 512], F32)) for i in range(8)]

        ones = sb("ones", [P, P], F32)
        ident = sb("ident", [P, P], F32)
        ident_b = sb("ident_b", [P, P], BF16)
        ones33 = sb("ones33", [BIAS_ROWS, P], F16)
        head_mask = sb("head_mask", [P, H], F32)
        group_mask = sb("group_mask", [P, G, HG], F32)
        neg_sel = sb("neg_sel", [MAX_ROWS, G, HG, M], BF16)
        expert_no = sb("expert_no", [P, T, E], F32)
        pick_expert = sb("pick_expert", [GATE_ROWS, E * P], F16)
        ident_h = sb("ident_h", [P, P], F16)
        x_sb = sb("x_sb", [P, B, T, D], F32)
        ctx_sb = sb("ctx_sb", [B * M, D], F32)
        wk_sb = sb("wk_sb", [P, D], F32)
        wvo_sb = sb("wvo_sb", [P, 2, D], F32)
        wq_sb = sb("wq_sb", [P, D], F32)
        smalls = sb("smalls", [R_ALL, D], F32)
        qkv_rows = sb("qkv_rows", [1, 3, D], F32)
        g_row = sb("g_row", [1, 2], F32)
        b2_sb = sb("b2_sb", [GATE_ROWS, D], F32)
        wkT = sb("wkT", [P, D], F32)
        turned = sb("turned", [P, C_SMALL + R_ALL], F32)
        wvT, woT, smallT = turned[:, 0:D], turned[:, D:2 * D], turned[:, C_SMALL:C_SMALL + R_ALL]
        ctxT = sb("ctxT", [P, B * M], F32)
        ctxT4 = sb("ctxT4", [P, B, HG, M], F32)
        sel33 = sb("sel33", [1, BIAS_ROWS], F32)
        bq33 = sb("bq33", [P, BIAS_ROWS], F32)
        tanh_g = sb("tanh_g", [P, 2], F32)
        gelu_first = sb("gelu_first", [P, 1], F32)
        half_gate = sb("half_gate", [P, 2], F32)
        b2_hi = sb("b2_hi", [GATE_ROWS, D], F16)
        b2_lo = sb("b2_lo", [GATE_ROWS, D], F16)
        wo32 = sb("wo32", [P, D], F32)
        wo_hi = sb("wo_hi", [P, D], F16)
        wo_lo = sb("wo_lo", [P, D], F16)
        k_bd = sb("k_bd", [P, B, H, M], F32)
        kq_hi = sb("kq_hi", [P, B, H * M], F16)
        kq_lo = sb("kq_lo", [P, B, H * M], F16)
        bias33 = sb("bias33", [BIAS_ROWS, B, H * M], F16)
        bias_col = sb("bias_col", [P, B, G], F32)
        v32 = sb("v32", [P, B, D], F32)
        vr = sb("vr", [P, B, G, VC], F16)
        v_lo = sb("v_lo", [P, B, G, HG * HD], F16)
        stats = sb("stats", [P, B, T, 6], F32)
        moments = sb("moments", [P, B, T, 2], F32)
        rstd = sb("rstd", [P, B, T], F32)
        neg_half = sb("neg_half", [P, T], F32)
        var_eps = sb("var_eps", [P, B, T], F32)
        xln = sb("xln", [P, B, T, D], F32)
        x_hi = sb("x_hi", [P, B, N], F16)
        x_lo = sb("x_lo", [P, B, N], F16)
        maxes = sb("maxes", [P, B, T, H], F32)
        max_hl = sb("max_hl", [P, B, T, MAX_ROWS], BF16)
        maxT = sb("maxT", [MAX_ROWS, B, N], BF16)
        p32 = sb("p32", [P, B, G, N], F32)
        p_hi = sb("p_hi", [P, B, G, N], F16)
        p_lo = sb("p_lo", [P, B, G, N], F16)
        r_den = sb("r_den", [P, B, T, G, HG], F32)
        o32 = xln
        o_hi = sb("o_hi", [P, B, N], F16)
        o_lo = sb("o_lo", [P, B, N], F16)
        x1 = sb("x1", [P, B, T, D], F32)
        zln = xln
        zT = k_bd[:, :, :, :].rearrange("p b h m -> p b (h m)")
        z_hi = sb("z_hi", [P, B, N], F16)
        z_lo = sb("z_lo", [P, B, N], F16)
        logits = sb("logits", [P, B, T, E], F32)
        r_a = sb("r_a", [P, B, T, E], F32)
        r_b = sb("r_b", [P, B, T, E], F32)
        pick1 = sb("pick1", [P, B, T, E], F32)
        pick2 = sb("pick2", [P, B, T, E], F32)
        top1 = sb("top1", [P, B, T], F32)
        top2 = sb("top2", [P, B, T], F32)
        least = sb("least", [P, B, T], F32)
        gap = sb("gap", [P, B, T], F32)
        th = sb("th", [P, B, T], F32)
        w_1 = sb("w_1", [P, B, T], F32)
        w_2 = sb("w_2", [P, B, T], F32)
        gates = sb("gates", [P, B, T, E], F32)
        gates_hl = sb("gates_hl", [P, B, T, GATE_ROWS], F16)
        gatesT = sb("gatesT", [GATE_ROWS, B, N], F16)
        w_scale = sb("w_scale", [P, I], F32)
        unit = sb("unit", [P, B * D], F32)
        raw1 = sb("raw1", [P, E, I], F32)
        raw2 = sb("raw2", [P, E, C * D], F32)
        w1_hi = sb("w1_hi", [P, E * I], F16)
        w1_lo = sb("w1_lo", [P, E * I], F16)
        w2_hi = sb("w2_hi", [P, E * C * D], F16)
        w2_lo = sb("w2_lo", [P, E * C * D], F16)
        gate_all = sb("gate_all", [P, E, N], F32)
        gate_now = gate_all
        h32 = [p32[:, 0], sb("h32", [P, C, N], F32)]
        h_hi = sb("h_hi", [P, 2, C, N], F16)
        h_lo = sb("h_lo", [P, 2, C, N], F16)
        gated = sb("gated", [P, 2, N], F32)
        accT = sb("accT", [P, B, N], F32)
        out_sb = xln

        ld_x = [sem(f"ld_x{b}") for b in range(B)]
        ld_ctx, ld_wk, ld_wvo, ld_small, ld_wq, ld_bk, ld_bq, ld_bv, ld_g, ld_b2 = (
            sem(n) for n in ("ld_ctx", "ld_wk", "ld_wvo", "ld_small", "ld_wq", "ld_bk", "ld_bq", "ld_bv", "ld_g",
                             "ld_b2"))
        ld_w = [sem(f"ld_w{e}") for e in range(E)]
        stored = sem("stored")
        pool_step, w_step, max_consts, neg_sel_done, group_mask_done, gate_consts = (
            sem(n) for n in ("pool_step", "w_step", "max_consts", "neg_sel_done", "group_mask_done", "gate_consts"))
        wkT_ps, ctxT_ps, bq33_ps, turned_ps, kT_ps, v_ps, g_ps = (
            sem(n) for n in ("wkT_ps", "ctxT_ps", "bq33_ps", "turned_ps", "kT_ps", "v_ps", "g_ps"))
        ident_done, head_mask_done, sel33_done, ones33_done = (
            sem(n) for n in ("ident_done", "head_mask_done", "sel33_done", "ones33_done"))
        wkT_done, ctxT_done, ctxT4_done, bq33_done, turned_done, tanh_done = (
            sem(n) for n in ("wkT_done", "ctxT_done", "ctxT4_done", "bq33_done", "turned_done", "tanh_done"))
        kbd_done, kq_ps, bias_row_ps, bias_col_ps = (
            sem(n) for n in ("kbd_done", "kq_ps", "bias_row_ps", "bias_col_ps"))
        kq_hi_done, kq_lo_done, bias_hi_done, bias_lo_done, bias_col_done, v_done = (
            sem(n) for n in ("kq_hi_done", "kq_lo_done", "bias_hi_done", "bias_lo_done", "bias_col_done",
                             "v_done"))
        v32_done, v_step, sums_done = sem("v32_done"), sem("v_step"), sem("sums_done")
        wo32_done, wo_hi_done, wo_lo_done = sem("wo32_done"), sem("wo_hi_done"), sem("wo_lo_done")
        dve_step = sem("dve_step")
        xln_done, xT_ps, x_hi_done, x_lo_done = (sem(n) for n in ("xln_done", "xT_ps", "x_hi_done", "x_lo_done"))
        var_done, rstd_done = sem("var_done"), sem("rstd_done")
        scores_ps, max_done, max_split, maxT_ps, maxT_done = (
            sem(n) for n in ("scores_ps", "max_done", "max_split", "maxT_ps", "maxT_done"))
        scoresT_ps, exp_done, p_hi_done, p_lo_done, p_lo_pool = (
            sem(n) for n in ("scoresT_ps", "exp_done", "p_hi_done", "p_lo_done", "p_lo_pool"))
        pv_ps, o_done, oT_ps, o_hi_done, o_lo_done, attn_ps = (
            sem(n) for n in ("pv_ps", "o_done", "oT_ps", "o_hi_done", "o_lo_done", "attn_ps"))
        zln_done, zT_ps, zT_done, z_hi_done, z_lo_done = (
            sem(n) for n in ("zln_done", "zT_ps", "zT_done", "z_hi_done", "z_lo_done"))
        logits_ps, logits_done, gap_done, th_done, gates_done, gatesT_ps, gatesT_done = (
            sem(n) for n in ("logits_ps", "logits_done", "gap_done", "th_done", "gates_done", "gatesT_ps",
                             "gatesT_done"))
        b2_done, b2_ps, acc_begun, gate_ps, gate_done = (
            sem(n) for n in ("b2_done", "b2_ps", "acc_begun", "gate_ps", "gate_done"))
        w_hi_act, w1_split, w2_split = sem("w_hi_act"), sem("w1_split"), sem("w2_split")
        up_ps, gelu_done, hi_dve, hi_act, h_split, down_ps, gated_done, acc_done = (
            sem(n) for n in ("up_ps", "gelu_done", "hi_dve", "hi_act", "h_split", "down_ps", "gated_done", "acc_done"))
        out_ps, out_done = sem("out_ps"), sem("out_done")

        tok = x.rearrange("b (p t) d -> p b t d", t=T)
        out_tok = out.rearrange("b (p t) d -> p b t d", t=T)

        wkT_bank = bank[3][:, 0:D]
        turned_bank = bank[5][:, 0:C_SMALL + R_ALL]
        ctxT_bank = bank[1][:, 0:B * M]
        bq33_bank = bank[6][:, 0:BIAS_ROWS]
        kT_bank = bank[2][:, 0:B * M]
        g_bank = bank[5][:, C_SMALL + R_ALL:C_SMALL + R_ALL + 2]
        bias_col_bank = [bank[5], bank[7]]
        v_bank = bank[0][:, 0:B * D].rearrange("p (b d) -> p b d", b=B)
        kq_bank = [bank[4], bank[7]]
        bias_row_bank = [bank[6], bank[6]]
        xT_bank = [bank[0], bank[1]]
        scores_bank = [bank[2], bank[3]]
        scoresT_bank = [bank[4], bank[5]]
        maxT_bank = [bank[5], bank[7]]
        half_bank = [bank[0], bank[1]]
        logits_bank = [bank[0], bank[1]]
        gatesT_bank = [bank[1], bank[0]]
        b2_bank = [bank[0], bank[1]]
        gate_bank = [bank[1], bank[0]]
        up_bank = [bank[6], bank[7], bank[4], bank[5]]
        down_bank = [bank[2], bank[3]]
        out0_bank = bank[1]
        out1_bank = [bank[0], bank[2]]

        HALVES = [slice(0, N // 2), slice(N // 2, N)]

        block = stack.enter_context(nc.Block())

        def part(start, size):
            return slice(start, start + size) if isinstance(start, int) else bass.ds(start, size)

        @block.sync
        def _(sp):
            sp.dma_start(wk_sb[:, :], Wk).then_inc(ld_wk, 16)
            sp.dma_start(x_sb[:, 0], tok[:, 0]).then_inc(ld_x[0], 16)
            sp.dma_start(qkv_rows[:, 1, :], bk.rearrange("(a d) -> a d", a=1)).then_inc(ld_bk, 16)
            sp.dma_start(wq_sb[:, :], Wq).then_inc(ld_wq, 16)
            sp.dma_start(qkv_rows[:, 0, :], bq.rearrange("(a d) -> a d", a=1)).then_inc(ld_bq, 16)
            sp.dma_start(x_sb[:, 1], tok[:, 1]).then_inc(ld_x[1], 16)
            sp.dma_start(wvo_sb[:, 0, :], Wv).then_inc(ld_wvo, 16)
            sp.dma_start(wvo_sb[:, 1, :], Wo).then_inc(ld_wvo, 16)
            sp.dma_start(smalls[R_WG:R_WG + E, :], Wg).then_inc(ld_small, 16)
            sp.dma_start(smalls[R_B1:R_B1 + E * C, :], b1.rearrange("e (c i) -> (e c) i", i=P)).then_inc(ld_small, 16)
            sp.dma_start(g_row[0:1, 0:1], g_xattn.rearrange("(a d) -> a d", a=1)).then_inc(ld_g, 16)
            sp.dma_start(g_row[0:1, 1:2], g_ffn.rearrange("(a d) -> a d", a=1)).then_inc(ld_g, 16)
            sp.dma_start(qkv_rows[:, 2, :], bv.rearrange("(a d) -> a d", a=1)).then_inc(ld_bv, 16)
            for e in range(E):
                sp.dma_start(raw1[:, e, :], W1[e]).then_inc(ld_w[e], 16)
                sp.dma_start(raw2[:, e, :].rearrange("p (c d) -> p c d", c=C),
                             W2[e].rearrange("(c p) d -> p c d", p=P)).then_inc(ld_w[e], 16)
            for r in (0, 32):
                sp.dma_start(b2_sb[r:r + E, :], b2).then_inc(ld_b2, 16)
            sp.wait_ge(out_done, 1)
            sp.dma_start(out_tok[:, 0], out_sb[:, 0]).then_inc(stored, 16)
            for half in range(2):
                tiles = slice(half * T // 2, (half + 1) * T // 2)
                sp.wait_ge(out_done, half + 2)
                sp.dma_start(out_tok[:, 1, tiles], out_sb[:, 1, tiles]).then_inc(stored, 16)
            sp.wait_ge(stored, 16 * 3)

        @block.gpsimd
        def _(pool):
            gp = nc.gpsimd
            gp.memset(ones[:, :], 1.0).then_inc(pool_step, 1)
            pool.wait_ge(pool_step, 1)
            gp.affine_select(out=ident[:, :], in_=ones[:, :], pattern=[[-1, P]], compare_op=ALU.is_equal, fill=0.0,
                             base=0, channel_multiplier=1).then_inc(ident_done, 1)
            gp.memset(sel33[:, :], 0.0).then_inc(pool_step, 1)
            gp.memset(head_mask[:, :], K_SCALE * HD ** -0.5).then_inc(pool_step, 1)
            gp.memset(neg_half[:, :], -0.5).then_inc(pool_step, 1)
            pool.wait_ge(pool_step, 4)
            for r in (0, 32):
                gp.memset(sel33[:, r:r + 1], 1.0).then_inc(sel33_done, 1)
            gp.affine_select(out=head_mask[:, :], in_=head_mask[:, :], pattern=[[-HD, H]], compare_op=ALU.is_ge,
                             fill=0.0, base=0, channel_multiplier=1).then_inc(pool_step, 1)
            pool.wait_ge(pool_step, 5)
            gp.affine_select(out=head_mask[:, :], in_=head_mask[:, :], pattern=[[HD, H]], compare_op=ALU.is_ge,
                             fill=0.0, base=HD - 1, channel_multiplier=-1).then_inc(head_mask_done, 1)
            gp.memset(ones33[:, :], 1.0).then_inc(ones33_done, 1)
            gp.memset(group_mask[:, :, :], 1.0).then_inc(pool_step, 1)
            gp.affine_select(out=ident_b[:, :], in_=ones[:, :], pattern=[[-1, P]], compare_op=ALU.is_equal, fill=0.0,
                             base=0, channel_multiplier=1).then_inc(max_consts, 1)
            gp.memset(max_hl[:, :, :, :], 0.0).then_inc(max_consts, 1)
            gp.memset(neg_sel[:, :, :, :], 0.0).then_inc(pool_step, 1)

            def rstd_of(n):
                pool.wait_ge(var_done, n + 1)
                gp.tensor_tensor(rstd[:, n % B, :], var_eps[:, n % B, :], neg_half[:, :],
                                 ALU.pow).then_inc(rstd_done, 1)

            rstd_of(0)
            pool.wait_ge(pool_step, 7)
            gp.affine_select(out=neg_sel[:, :, :, :], in_=neg_sel[:, :, :, :], pattern=[[-HG, G], [-1, HG], [0, M]],
                             compare_op=ALU.not_equal, fill=-1.0, base=0, channel_multiplier=1).then_inc(pool_step, 1)
            gp.affine_select(out=group_mask[:, :, :], in_=group_mask[:, :, :], pattern=[[0, G], [-M, HG]],
                             compare_op=ALU.is_ge, fill=0.0, base=0, channel_multiplier=1).then_inc(pool_step, 1)
            gp.memset(w_scale[:, :], W_SCALE).then_inc(pool_step, 1)
            gp.memset(unit[:, :], 1.0).then_inc(pool_step, 1)
            pool.wait_ge(pool_step, 9)
            gp.affine_select(out=neg_sel[:, :, :, :], in_=neg_sel[:, :, :, :], pattern=[[-HG, G], [-1, HG], [0, M]],
                             compare_op=ALU.not_equal, fill=-1.0, base=-32,
                             channel_multiplier=1).then_inc(neg_sel_done, 1)
            gp.affine_select(out=group_mask[:, :, :], in_=group_mask[:, :, :], pattern=[[0, G], [M, HG]],
                             compare_op=ALU.is_ge, fill=0.0, base=M - 1,
                             channel_multiplier=-1).then_inc(group_mask_done, 1)
            pool.wait_ge(pool_step, 11)

            def split_weights(e, *which):
                pool.wait_ge(ld_w[e], 32)
                for n in which or range(2):
                    raw, hi, lo, done = ((raw1, w1_hi, w1_lo, w1_split), (raw2, w2_hi, w2_lo, w2_split))[n]
                    at = slice(e * I, (e + 1) * I)
                    pool.wait_ge(w_hi_act, 2 * e + n + 1)
                    gp.tensor_tensor(raw[:, e, :], raw[:, e, :], w_scale[:, :], ALU.mult).then_inc(w_step, 1)
                    pool.wait_ge(w_step, 2 * e + n + 1)
                    gp.tensor_tensor(lo[:, at], raw[:, e, :], hi[:, at], ALU.subtract).then_inc(done, 1)

            split_weights(0, 0)
            rstd_of(1)
            split_weights(0, 1)

            heads = [P, B, H, HD]
            pool.wait_ge(group_mask_done, 1)
            pool.wait_ge(v32_done, 1)
            v_ = v32[:, :, :].rearrange("p b (h d) -> p b h d", h=H)
            gp.tensor_tensor(v_, v_, group_mask[:, :, :].rearrange("p g h -> p (g h)").unsqueeze(1).unsqueeze(3)
                             .to_broadcast(heads), ALU.mult).then_inc(v_step, 1)
            v_ = v32[:, :, :].rearrange("p b (g c) -> p (b g) c", g=G)
            v_hi = vr[:, :, :, 0:HG * HD].rearrange("p b g c -> p (b g) c")
            pool.wait_ge(v_step, 1)
            gp.tensor_tensor(v_hi, v_, unit[:, :].rearrange("p (u c) -> p u c", c=HG * HD),
                             ALU.mult).then_inc(v_step, 1)
            pool.wait_ge(v_step, 2)
            gp.tensor_tensor(v_lo[:, :, :, :].rearrange("p b g c -> p (b g) c"), v_, v_hi,
                             ALU.subtract).then_inc(v_done, 1)

            split_weights(1)
            gp.affine_select(out=ident_h[:, :], in_=ones[:, :], pattern=[[-1, P]], compare_op=ALU.is_equal, fill=0.0,
                             base=0, channel_multiplier=1).then_inc(gate_consts, 1)
            gp.memset(gates_hl[:, :, :, :], 0.0).then_inc(gate_consts, 1)
            gp.memset(b2_hi[:, :], 0.0).then_inc(gate_consts, 1)
            gp.memset(b2_lo[:, :], 0.0).then_inc(gate_consts, 1)
            gp.iota(expert_no[:, :, :], [[0, T], [1, E]], base=0, channel_multiplier=0,
                    allow_small_or_imprecise_dtypes=True).then_inc(gate_consts, 1)
            split_weights(2)
            rstd_of(2)
            gp.memset(pick_expert[:, :], 0.0).then_inc(pool_step, 1)
            pool.wait_ge(pool_step, 12)
            gp.affine_select(out=pick_expert[:, :], in_=pick_expert[:, :], pattern=[[-1, E], [0, P]],
                             compare_op=ALU.not_equal, fill=1.0, base=0, channel_multiplier=1).then_inc(pool_step, 1)
            pool.wait_ge(pool_step, 13)
            gp.affine_select(out=pick_expert[:, :], in_=pick_expert[:, :], pattern=[[-1, E], [0, P]],
                             compare_op=ALU.not_equal, fill=1.0, base=-32,
                             channel_multiplier=1).then_inc(gate_consts, 1)
            split_weights(3)
            split_weights(4)
            for g in range(2, G):
                pool.wait_ge(p_hi_done, G + g + 1)
                gp.tensor_tensor(p_lo[:, 1, g, :], p32[:, 1, g, :], p_hi[:, 1, g, :], ALU.subtract).then_inc(
                    p_lo_pool, 1)
            split_weights(5)
            split_weights(6)
            split_weights(7)

            def add_step(b, s, k):
                pool.wait_ge(acc_done, s)
                pool.wait_ge(gated_done, s + 1)
                gp.tensor_tensor(accT[:, b, :], accT[:, b, :], gated[:, k, :], ALU.add).then_inc(acc_done, 1)

            rstd_of(3)
            for e in range(DVE_ADDS, E):
                add_step(0, e, e % 2)

            pool.wait_ge(acc_begun, B)
            with pool.Fori(0, E // 2 - 1) as pair:
                for k in range(2):
                    add_step(1, E + 2 * pair + k, k)
            add_step(1, S - 2, 0)

        @block.scalar
        def _(act):
            ac = nc.scalar
            act.dma_start(ctx_sb[:, :], ctx_in.rearrange("b m d -> (b m) d")).then_inc(ld_ctx, 16)

            def halves_high(dst, b, ready, done):
                for half, cols in enumerate(HALVES):
                    high_half(dst[:, b, cols], half_bank[half][:, 0:N // 2], ready, 2 * b + half + 1, done)

            def high_half(dst, src, ready, value, done):
                act.wait_ge(ready, value)
                ac.copy(dst, src).then_inc(done, 1)

            def weights_high(e, *which):
                act.wait_ge(ld_w[e], 32)
                for n in which or range(2):
                    raw, hi = ((raw1, w1_hi), (raw2, w2_hi))[n]
                    ac.activation(hi[:, e * I:(e + 1) * I], raw[:, e, :], ACT.Copy, scale=W_SCALE).then_inc(w_hi_act, 1)

            def kq_high(b):
                high_half(kq_hi[:, b, :], kq_bank[b][:, :], kq_ps, b + 1, kq_hi_done)

            def bias_high(b):
                high_half(bias33[:, b, :], bias_row_bank[b][0:BIAS_ROWS, :], bias_row_ps, b + 1, bias_hi_done)

            def bias_columns(b):
                act.wait_ge(bias_col_ps, b + 1)
                ac.activation(bias_col[:, b, :], bias_col_bank[b][:, 0:G], ACT.Copy, bias=P_LOG_SCALE,
                              scale=1.0 / K_SCALE).then_inc(bias_col_done, 1)

            def max_rows(b):
                act.wait_ge(maxT_ps, b + 1)
                ac.copy(maxT[:, b, :], maxT_bank[b][0:MAX_ROWS, 0:N // 2].bitcast(BF16)).then_inc(maxT_done, 1)

            def exponentials(b, g):
                act.wait_ge(scoresT_ps, b * G + g + 1)
                ac.activation(p32[:, b, g, :], scoresT_bank[g % 2][:, :], ACT.Exp, bias=bias_col[:, b, g:g + 1],
                              scale=1.0 / K_SCALE).then_inc(exp_done, 1)

            def p_high(b, g):
                act.wait_ge(exp_done, b * G + g + 1)
                ac.copy(p_hi[:, b, g, :], p32[:, b, g, :]).then_inc(p_hi_done, 1)

            def o_high(b):
                halves_high(o_hi, b, oT_ps, o_hi_done)

            def z_high(b):
                halves_high(z_hi, b, zT_ps, z_hi_done)

            def z_whole(b):
                act.wait_ge(z_lo_done, 2 * (b + 1))
                for half, cols in enumerate(HALVES):
                    ac.copy(zT[:, b, cols], half_bank[half][:, 0:N // 2]).then_inc(zT_done, 1)

            def router_tanh(b):
                act.wait_ge(gap_done, b + 1)
                ac.activation(th[:, b, :], gap[:, b, :], ACT.Tanh, scale=0.5).then_inc(th_done, 1)

            def gate_rows(b):
                act.wait_ge(gatesT_ps, b + 1)
                ac.copy(gatesT[:, b, :], gatesT_bank[b][0:GATE_ROWS, 0:N // 2].bitcast(F16)).then_inc(gatesT_done, 1)

            def begin_acc(b):
                act.wait_ge(b2_ps, b + 1)
                ac.activation(accT[:, b, :], b2_bank[b][:, :], ACT.Copy,
                              scale=1.0 / (GATE_SCALE * B2_SCALE)).then_inc(acc_begun, 1)

            def keep_gates(*experts):
                for e in experts:
                    act.wait_ge(gate_ps, e + 1)
                    ac.copy(gate_all[:, e, :], gate_bank[e % 2][:, :]).then_inc(gate_done, 1)

            def keep_gates1(s, k):
                act.wait_ge(gated_done, s - 1)
                act.wait_ge(gate_ps, s + 1)
                ac.copy(gate_now[:, k, :], gate_bank[1][:, :]).then_inc(gate_done, 1)

            def gelus(s, e, k, *chunks):
                if not isinstance(s, int) or s >= 2:
                    act.wait_ge(h_split, 2 * s - 2)
                for c in chunks or range(C):
                    act.wait_ge(up_ps, C * s + c + 1)
                    act.wait_ge(turned_done, 1)
                    ac.activation(h32[k][:, c, :], up_bank[c][:, :], ACT.Gelu,
                                  bias=smallT[:, part(R_B1 + e * C + c, 1)],
                                  scale=1.0 / W_SCALE).then_inc(gelu_done, 1)

            def hidden_high(s, k):
                if not isinstance(s, int) or s >= 2:
                    act.wait_ge(down_ps, s - 1)
                act.wait_ge(gelu_done, C * s + C)
                ac.activation(h_hi[:, k, 2:4, :], h32[k][:, 2:4, :], ACT.Copy, scale=H_SCALE).then_inc(hi_act, 1)

            act.wait_ge(wkT_ps, 1)
            ac.copy(wkT[:, :], wkT_bank).then_inc(wkT_done, 1)
            act.wait_ge(ctxT_ps, 1)
            ac.copy(ctxT[:, :], ctxT_bank).then_inc(ctxT_done, 1)
            act.wait_ge(bq33_ps, 1)
            ac.copy(bq33[:, :], bq33_bank).then_inc(bq33_done, 1)
            kq_high(0)
            high_half(x_hi[:, 0, :], xT_bank[0][:, :], xT_ps, 1, x_hi_done)
            bias_high(0)
            act.wait_ge(turned_ps, 1)
            ac.copy(turned[:, :], turned_bank).then_inc(turned_done, 1)
            weights_high(0)
            act.wait_ge(g_ps, 1)
            ac.activation(tanh_g[:, :], g_bank, ACT.Tanh).then_inc(tanh_done, 1)
            act.wait_ge(tanh_done, 1)
            ac.activation(wo32[:, :], woT, ACT.Copy, scale=tanh_g[:, 0:1]).then_inc(wo32_done, 1)
            weights_high(1)
            bias_columns(0)
            act.wait_ge(wo32_done, 1)
            ac.activation(wo_hi[:, :], wo32[:, :], ACT.Copy, scale=WO_SCALE).then_inc(wo_hi_done, 1)
            act.wait_ge(group_mask_done, 1)
            for b in range(B):
                s_ = ac.activation(vr[:, b, :, HG * HD:VC], group_mask[:, :, :], ACT.Copy, scale=1.0 / O_SCALE)
            s_.then_inc(sums_done, 1)
            kq_high(1)
            max_rows(0)
            bias_high(1)
            act.wait_ge(v_ps, 1)
            ac.copy(v32[:, :, :], v_bank).then_inc(v32_done, 1)
            act.wait_ge(bias_col_done, 1)
            exponentials(0, 0)
            p_high(0, 0)
            for g in range(1, G):
                exponentials(0, g)
                p_high(0, g)
            weights_high(2)
            weights_high(3)
            bias_columns(1)
            o_high(0)
            weights_high(4)
            weights_high(5, 0)
            max_rows(1)
            act.wait_ge(bias_col_done, 2)
            for g in range(G):
                exponentials(1, g)
                if g < 1:
                    p_high(1, g)
            ac.activation(gelu_first[:, :], ones[:, 0:1], ACT.Gelu)
            z_whole(0)
            p_high(1, 1)
            p_high(1, 2)
            gelus(0, 0, 0)
            hidden_high(0, 0)
            weights_high(5, 1)
            p_high(1, 3)
            gelus(1, 1, 1)
            hidden_high(1, 1)
            weights_high(6, 0)
            router_tanh(0)
            gelus(2, 2, 0)
            hidden_high(2, 0)
            weights_high(6, 1)
            gate_rows(0)
            begin_acc(0)
            keep_gates(0, 1)
            gelus(3, 3, 1)
            hidden_high(3, 1)
            keep_gates(2, 3)
            gelus(4, 4, 0, 0, 1)
            keep_gates(4)
            gelus(4, 4, 0, 2, 3)
            keep_gates(5)
            hidden_high(4, 0)
            keep_gates(6, 7)
            weights_high(7, 0)
            gelus(5, 5, 1)
            o_high(1)
            hidden_high(5, 1)
            weights_high(7, 1)
            gelus(6, 6, 0)
            hidden_high(6, 0)
            gelus(7, 7, 1, 0, 1)
            z_high(1)
            gelus(7, 7, 1, 2, 3)
            z_whole(1)
            hidden_high(7, 1)
            gelus(E, 0, 0)
            router_tanh(1)
            hidden_high(E, 0)
            gelus(E + 1, 1, 1)
            hidden_high(E + 1, 1)
            gate_rows(1)
            begin_acc(1)
            keep_gates1(E, 0)
            with act.Fori(0, E // 2 - 1) as pair:
                for k in range(2):
                    s, e = E + 2 * pair + k, 2 * pair + k
                    gelus(s + 2, e + 2, k)
                    hidden_high(s + 2, k)
                    keep_gates1(s + 1, 1 - k)
            keep_gates1(S - 1, 1)

        @block.tensor
        def _(pe):
            te = nc.tensor

            def product(out_, a_hi, a_lo, b_hi, b_lo, start=True, stop=True):
                te.matmul(out_, a_hi, b_hi, start=start, stop=False, skip_group_check=True)
                te.matmul(out_, a_hi, b_lo, start=False, stop=False, skip_group_check=True)
                return te.matmul(out_, a_lo, b_hi, start=False, stop=stop, skip_group_check=True)

            def transpose_x(b):
                pe.wait_ge(xln_done, 2 * (b + 1))
                for t in range(T):
                    t_ = te.transpose(xT_bank[b][:, t * P:(t + 1) * P], xln[:, b, t, :], ident[:, :])
                t_.then_inc(xT_ps, 1)

            def keys(b):
                pe.wait_ge(kbd_done, b + 1)
                te.matmul(kq_bank[b][:, :], wq_sb[:, :], k_bd[:, b].rearrange("p h m -> p (h m)"), start=True,
                          stop=True).then_inc(kq_ps, 1)

            def bias_row(b):
                te.matmul(bias_row_bank[b][0:BIAS_ROWS, :], bq33[:, :], k_bd[:, b].rearrange("p h m -> p (h m)"),
                          start=True, stop=True).then_inc(bias_row_ps, 1)

            def scores(b, *tiles):
                for t in tiles:
                    if t == 0:
                        pe.wait_ge(x_hi_done, b + 1)
                        pe.wait_ge(x_lo_done, b + 1)
                        pe.wait_ge(kq_hi_done, b + 1)
                        pe.wait_ge(kq_lo_done, b + 1)
                    n = b * T + t
                    if n >= 2:
                        pe.wait_ge(max_done, n - 1)
                    rows = slice(t * P, (t + 1) * P)
                    product(scores_bank[n % 2][:, :], x_hi[:, b, rows], x_lo[:, b, rows], kq_hi[:, b, :],
                            kq_lo[:, b, :], stop=False)
                    if t == 0:
                        pe.wait_ge(bias_lo_done, b + 1)
                    te.matmul(scores_bank[n % 2][:, :], ones33[:, :], bias33[:, b, :], start=False, stop=True,
                              skip_group_check=True).then_inc(scores_ps, 1)

            def bias_columns(b):
                pe.wait_ge(bias_lo_done, b + 1)
                for g in range(G):
                    t_ = te.matmul(bias_col_bank[b][:, g:g + 1], bias33[:, b, g * P:(g + 1) * P], ones33[:, 0:1],
                                   start=True, stop=True)
                t_.then_inc(bias_col_ps, 1)

            def transpose_max(b):
                pe.wait_ge(max_split, b + 1)
                pe.wait_ge(bias_col_done, b + 1)
                for t in range(T):
                    t_ = te.transpose(maxT_bank[b][0:MAX_ROWS, t * P // 2:(t + 1) * P // 2].bitcast(BF16),
                                      max_hl[:, b, t, :], ident_b[:, :])
                t_.then_inc(maxT_ps, 1)

            def begin_transposed(b, g):
                n = b * G + g
                if n >= 2:
                    pe.wait_ge(exp_done, n - 1)
                rows = slice(g * P, (g + 1) * P)
                product(scoresT_bank[n % 2][:, :], kq_hi[:, b, rows], kq_lo[:, b, rows], x_hi[:, b, :],
                        x_lo[:, b, :], stop=False)

            def less_maxima(b, g):
                pe.wait_ge(maxT_done, b + 1)
                pe.wait_ge(neg_sel_done, 1)
                te.matmul(scoresT_bank[(b * G + g) % 2][:, :], neg_sel[:, g].rearrange("p h m -> p (h m)"),
                          maxT[:, b, :], start=False, stop=True, skip_group_check=True).then_inc(scoresT_ps, 1)

            def scores_transposed(b, *groups):
                for g in groups:
                    begin_transposed(b, g)
                    less_maxima(b, g)

            def values(b):
                pe.wait_ge(p_hi_done, (b + 1) * G)
                if b == 0:
                    pe.wait_ge(p_lo_done, G)
                else:
                    pe.wait_ge(p_lo_done, G + 2)
                    pe.wait_ge(p_lo_pool, 2)
                for half in range(2):
                    for u in range(2):
                        t = 2 * half + u
                        rows = slice(t * P, (t + 1) * P)
                        for g in range(G):
                            at = (u * G + g) * VC
                            first = u == 0 and g == 0
                            last = u == 1 and g == G - 1
                            full = half_bank[half][:, at:at + VC]
                            te.matmul(full, p_hi[:, b, g, rows], vr[:, b, g, :], start=first, stop=False,
                                      skip_group_check=True)
                            te.matmul(full[:, 0:HG * HD], p_hi[:, b, g, rows], v_lo[:, b, g, :], start=False,
                                      stop=False, skip_group_check=True)
                            t_ = te.matmul(full, p_lo[:, b, g, rows], vr[:, b, g, :], start=False, stop=last,
                                           skip_group_check=True)
                    t_.then_inc(pv_ps, 1)

            def transpose_halves(b, src, ready, done):
                for half in range(2):
                    pe.wait_ge(ready, 2 * b + half + 1)
                    for u in range(2):
                        t_ = te.transpose(half_bank[half][:, u * P:(u + 1) * P], src[:, b, 2 * half + u, :],
                                          ident[:, :])
                    t_.then_inc(done, 1)

            def attention_out(b):
                for half in range(2):
                    pe.wait_ge(o_hi_done, 2 * b + half + 1)
                    pe.wait_ge(o_lo_done, 2 * b + half + 1)
                    for u in range(2):
                        rows = slice((2 * half + u) * P, (2 * half + u + 1) * P)
                        t_ = product(half_bank[half][:, u * P:(u + 1) * P], o_hi[:, b, rows], o_lo[:, b, rows],
                                     wo_hi[:, :], wo_lo[:, :], start=(u == 0), stop=(u == 1))
                    t_.then_inc(attn_ps, 1)

            def router(b):
                pe.wait_ge(zT_done, 2 * (b + 1))
                for t in range(T):
                    t_ = te.matmul(logits_bank[b][:, t * E:(t + 1) * E], zT[:, b, t * P:(t + 1) * P],
                                   smallT[:, R_WG:R_WG + E], start=True, stop=True)
                t_.then_inc(logits_ps, 1)

            def transpose_gates(b):
                pe.wait_ge(gates_done, b + 1)
                pe.wait_ge(z_lo_done, 2 * (b + 1))
                for t in range(T):
                    t_ = te.transpose(gatesT_bank[b][0:GATE_ROWS, t * P // 2:(t + 1) * P // 2].bitcast(F16),
                                      gates_hl[:, b, t, :], ident_h[:, :])
                t_.then_inc(gatesT_ps, 1)

            def b2_sum(b):
                pe.wait_ge(b2_done, 1)
                pe.wait_ge(gatesT_done, b + 1)
                te.matmul(b2_bank[b][:, :], b2_hi[:, :], gatesT[:, b, :], start=True, stop=False)
                te.matmul(b2_bank[b][:, :], b2_lo[:, :], gatesT[:, b, :], start=False, stop=True).then_inc(b2_ps, 1)

            def spread_gates0(*experts):
                for e in experts:
                    if e == 1:
                        pe.wait_ge(acc_begun, 1)
                    elif e > 1:
                        pe.wait_ge(gate_done, e - 1)
                    te.matmul(gate_bank[e % 2][:, :], pick_expert[:, e * P:(e + 1) * P], gatesT[:, 0, :], start=True,
                              stop=True).then_inc(gate_ps, 1)

            def spread_gates1(s, e):
                pe.wait_ge(gate_done, s)
                te.matmul(gate_bank[1][:, :], pick_expert[:, part(e * P, P)], gatesT[:, 1, :], start=True,
                          stop=True).then_inc(gate_ps, 1)

            def up(s, b, e, *chunks):
                for c in chunks or range(C):
                    if not isinstance(s, int) or s >= 1:
                        pe.wait_ge(gelu_done, C * s - C + c + 1)
                    cols = part(e * I + c * P, P)
                    product(up_bank[c][:, :], w1_hi[:, cols], w1_lo[:, cols], z_hi[:, b, :],
                            z_lo[:, b, :]).then_inc(up_ps, 1)

            def first_up():
                pe.wait_ge(w1_split, 1)
                chunk_cols = [slice(c * P, (c + 1) * P) for c in range(2)]
                for c, cols in enumerate(chunk_cols):
                    te.matmul(up_bank[c][:, :], w1_hi[:, cols], z_hi[:, 0, :], start=True, stop=False)
                    te.matmul(up_bank[c][:, :], w1_lo[:, cols], z_hi[:, 0, :], start=False, stop=False)
                pe.wait_ge(z_lo_done, 2)
                for c, cols in enumerate(chunk_cols):
                    te.matmul(up_bank[c][:, :], w1_hi[:, cols], z_lo[:, 0, :], start=False,
                              stop=True).then_inc(up_ps, 1)

            def down(s, e, k, *chunks):
                chunks = chunks or range(C)
                if 0 in chunks and (not isinstance(s, int) or s >= 2):
                    pe.wait_ge(gated_done, s - 1)
                for c in chunks:
                    if c % 2 == 0:
                        pe.wait_ge(h_split, 2 * s + c // 2 + 1)
                    cols = part(e * C * D + c * D, D)
                    t_ = product(down_bank[k][:, :], w2_hi[:, cols], w2_lo[:, cols], h_hi[:, k, c, :], h_lo[:, k, c, :],
                                 start=(c == 0), stop=(c == C - 1))
                if C - 1 in chunks:
                    t_.then_inc(down_ps, 1)

            def up0(e, *chunks):
                pe.wait_ge(w1_split, e + 1)
                up(e, 0, e, *chunks)

            def down0(e):
                pe.wait_ge(w2_split, e + 1)
                down(e, e, e % 2)

            def transpose_out0():
                pe.wait_ge(acc_done, E)
                pe.wait_ge(acc_begun, B)
                for t in range(T):
                    rows = slice(t * P, (t + 1) * P)
                    t_ = te.transpose(out0_bank[:, rows], accT[:, 0, rows], ident[:, :])
                t_.then_inc(out_ps, 1)

            def turn_back(src, start, stop):
                for half in range(2):
                    if stop:
                        pe.wait_ge(gated_done, S + half)
                    for u in range(2):
                        rows = slice((2 * half + u) * P, (2 * half + u + 1) * P)
                        t_ = te.matmul(out1_bank[half][:, u * P:(u + 1) * P], src[:, rows], ident[:, :],
                                       start=(start and u == 0), stop=(stop and u == 1), skip_group_check=True)
                    if stop:
                        t_.then_inc(out_ps, 1)

            pe.wait_ge(ident_done, 1)
            pe.wait_ge(ld_wk, 16)
            te.transpose(wkT_bank, wk_sb[:, :], ident[:, :]).then_inc(wkT_ps, 1)
            pe.wait_ge(ld_ctx, 16)
            te.transpose(ctxT_bank, ctx_sb[:, :], ident[0:B * M, 0:B * M]).then_inc(ctxT_ps, 1)
            pe.wait_ge(wkT_done, 1)
            pe.wait_ge(ctxT_done, 1)
            te.matmul(kT_bank, wkT[:, :], ctxT[:, :], start=True, stop=False)
            pe.wait_ge(ld_bk, 16)
            te.matmul(kT_bank, qkv_rows[:, 1, :], ones[0:1, 0:B * M], start=False, stop=True).then_inc(kT_ps, 1)
            pe.wait_ge(sel33_done, 2)
            pe.wait_ge(ld_bq, 16)
            te.matmul(bq33_bank, qkv_rows[:, 0, :], sel33[:, :], start=True, stop=True).then_inc(bq33_ps, 1)
            pe.wait_ge(ld_wq, 16)
            keys(0)
            transpose_x(0)
            pe.wait_ge(bq33_done, 1)
            bias_row(0)
            pe.wait_ge(ld_wvo, 32)
            for w in range(2):
                te.transpose(turned_bank[:, w * D:(w + 1) * D], wvo_sb[:, w, :], ident[:, :])
            pe.wait_ge(ld_small, 32)
            te.transpose(turned_bank[:, C_SMALL:C_SMALL + R_ALL], smalls[:, :],
                         ident[0:R_ALL, 0:R_ALL]).then_inc(turned_ps, 1)
            pe.wait_ge(kbd_done, 2)
            pe.wait_ge(ones33_done, 1)
            scores(0, 0, 1)
            pe.wait_ge(ld_g, 32)
            pe.wait_ge(turned_done, 1)
            te.matmul(g_bank, ones[0:1, :], g_row[:, :], start=True, stop=True).then_inc(g_ps, 1)
            scores(0, 2, 3)
            pe.wait_ge(tanh_done, 1)
            bias_columns(0)
            keys(1)
            pe.wait_ge(bias_lo_done, 1)
            bias_row(1)
            pe.wait_ge(max_consts, 2)
            transpose_max(0)
            pe.wait_ge(ctxT4_done, 1)
            pe.wait_ge(ld_bv, 16)
            for b in range(B):
                te.matmul(v_bank[:, b, :], ctxT4[:, b].rearrange("p h m -> p (h m)"), wvT, start=True, stop=False)
                t_ = te.matmul(v_bank[:, b, :], ones[0:1, :], qkv_rows[:, 2, :], start=False, stop=True)
            t_.then_inc(v_ps, 1)
            scores_transposed(0, 0)
            transpose_x(1)
            scores_transposed(0, 1, 2)
            scores(1, 0)
            scores_transposed(0, 3)
            scores(1, 1, 2)
            pe.wait_ge(v_done, 1)
            pe.wait_ge(sums_done, 1)
            values(0)
            bias_columns(1)
            scores(1, 3)
            transpose_halves(0, o32, o_done, oT_ps)
            pe.wait_ge(wo_lo_done, 1)
            attention_out(0)
            begin_transposed(1, 0)
            transpose_max(1)
            begin_transposed(1, 1)
            for g in range(2):
                less_maxima(1, g)
            scores_transposed(1, 2, 3)
            transpose_halves(0, zln, zln_done, zT_ps)
            pe.wait_ge(z_hi_done, 2)
            first_up()
            pe.wait_ge(exp_done, B * G)
            up0(0, 2)
            router(0)
            up0(0, 3)
            up0(1)
            down0(0)
            up0(2)
            down0(1)
            pe.wait_ge(gate_consts, 6)
            transpose_gates(0)
            up0(3, 0, 1)
            b2_sum(0)
            spread_gates0(0)
            up0(3, 2, 3)
            spread_gates0(1)
            down0(2)
            spread_gates0(2, 3)
            up0(4, 0, 1)
            spread_gates0(4)
            up0(4, 2, 3)
            spread_gates0(5)
            down0(3)
            spread_gates0(6, 7)
            up0(5, 0, 1)
            pe.wait_ge(gate_done, E)
            values(1)
            up0(5, 2, 3)
            transpose_halves(1, o32, o_done, oT_ps)
            down0(4)
            attention_out(1)
            up0(6)
            down0(5)
            up0(7, 0, 1)
            transpose_halves(1, zln, zln_done, zT_ps)
            up0(7, 2, 3)
            down0(6)
            router(1)
            pe.wait_ge(z_hi_done, 4)
            pe.wait_ge(z_lo_done, 4)
            up(E, 1, 0)
            down0(7)
            up(E + 1, 1, 1)
            down(E, 0, 0, 0, 1)
            transpose_gates(1)
            down(E, 0, 0, 2, 3)
            b2_sum(1)
            spread_gates1(E, 0)
            with pe.Fori(0, E // 2 - 1) as pair:
                for k in range(2):
                    s, e = E + 2 * pair + k, 2 * pair + k
                    up(s + 2, 1, e + 2)
                    spread_gates1(s + 1, e + 1)
                    down(s + 1, e + 1, 1 - k)
            spread_gates1(S - 1, E - 1)
            transpose_out0()
            down(S - 1, E - 1, 1)
            pe.wait_ge(acc_done, S - 1)
            pe.wait_ge(gate_done, S)
            turn_back(accT[:, 1, :], True, False)
            turn_back(gated[:, 1, :], False, True)

        @block.vector
        def _(dve):
            ve = nc.vector
            count = [0]

            def link(ins):
                count[0] += 1
                ins.then_inc(dve_step, 1)
                dve.wait_ge(dve_step, count[0])

            def stats_of(src, b, *tiles):
                for t in tiles:
                    i_ = ve.bn_stats(stats[:, b, t, :], src[:, b, t, :])
                return i_

            def moments_of(b, last_stats):
                link(last_stats)
                for t in range(T):
                    i_ = ve.bn_aggr(moments[:, b, t, :], stats[:, b, t, :])
                link(i_)
                ve.tensor_scalar(var_eps[:, b, :], moments[:, b, :, 1], LN_EPS, None, ALU.add).then_inc(var_done, 1)

            def normalise(dst, src, b, value, done):
                dve.wait_ge(rstd_done, value)
                for t in range(T):
                    i_ = ve.tensor_scalar(dst[:, b, t, :], src[:, b, t, :], moments[:, b, t, 0:1],
                                          rstd[:, b, t:t + 1], ALU.subtract, ALU.mult)
                    if t % 2 == 1:
                        i_.then_inc(done, 1)

            def apart(b):
                ve.tensor_tensor(k_bd[:, b], kT_bank[:, b * M:(b + 1) * M].unsqueeze(1).to_broadcast([P, H, M]),
                                 head_mask[:, :].unsqueeze(2).to_broadcast([P, H, M]), ALU.mult).then_inc(kbd_done, 1)

            def low_half(dst, src, high, done, value):
                dve.wait_ge(done, value)
                return ve.tensor_tensor(dst, src, high, ALU.subtract)

            def x_low(b):
                low_half(x_lo[:, b, :], xT_bank[b][:, :], x_hi[:, b, :], x_hi_done, b + 1).then_inc(x_lo_done, 1)

            def keys_low(b):
                low_half(kq_lo[:, b, :], kq_bank[b][:, :], kq_hi[:, b, :], kq_hi_done, b + 1).then_inc(kq_lo_done, 1)

            def bias_low(b):
                low_half(bias33[32:33, b, :], bias_row_bank[b][32:33, :], bias33[32:33, b, :], bias_hi_done,
                         b + 1).then_inc(bias_lo_done, 1)

            def maxima(b, *tiles):
                for t in tiles:
                    n = b * T + t
                    dve.wait_ge(scores_ps, n + 1)
                    ve.tensor_reduce(maxes[:, b, t, :], scores_bank[n % 2][:, :].rearrange("p (h m) -> p h m", h=H),
                                     AX.X, ALU.max).then_inc(max_done, 1)

            def split_maxima(b):
                dve.wait_ge(max_done, T * (b + 1))
                link(ve.tensor_copy(max_hl[:, b, :, 0:H], maxes[:, b, :, :]))
                ve.tensor_tensor(max_hl[:, b, :, 32:32 + H], maxes[:, b, :, :], max_hl[:, b, :, 0:H],
                                 ALU.subtract).then_inc(max_split, 1)

            def wo_low():
                dve.wait_ge(wo_hi_done, 1)
                ve.scalar_tensor_tensor(out=wo_lo[:, :], in0=wo32[:, :], scalar=WO_SCALE, in1=wo_hi[:, :],
                                        op0=ALU.mult, op1=ALU.subtract).then_inc(wo_lo_done, 1)

            def router_constants():
                dve.wait_ge(tanh_done, 1)
                ve.tensor_scalar(half_gate[:, 0:1], tanh_g[:, 1:2], 0.5 * GATE_SCALE, None, ALU.mult)
                ve.tensor_scalar(half_gate[:, 1:2], tanh_g[:, 1:2], -0.5 * GATE_SCALE, None, ALU.mult)
                dve.wait_ge(ld_b2, 32)
                for r in (0, 32):
                    rows = slice(r, r + E)
                    i_ = ve.tensor_scalar(b2_hi[rows, :], b2_sb[rows, :], B2_SCALE, None, ALU.mult)
                link(i_)
                for r in (0, 32):
                    rows = slice(r, r + E)
                    i_ = ve.scalar_tensor_tensor(out=b2_lo[rows, :], in0=b2_sb[rows, :], scalar=B2_SCALE,
                                                 in1=b2_hi[rows, :], op0=ALU.mult, op1=ALU.subtract)
                i_.then_inc(b2_done, 1)

            def p_low(b, g):
                dve.wait_ge(p_hi_done, b * G + g + 1)
                ve.tensor_tensor(p_lo[:, b, g, :], p32[:, b, g, :], p_hi[:, b, g, :],
                                 ALU.subtract).then_inc(p_lo_done, 1)

            def normalise_heads(b, half):
                dve.wait_ge(pv_ps, 2 * b + half + 1)
                sums = half_bank[half][:, 0:2 * G * VC].rearrange("p (u c) -> p u c", c=VC)
                r_ = r_den[:, b, 2 * half:2 * half + 2].rearrange("p t g h -> p (t g) h")
                link(ve.reciprocal(r_, sums[:, :, HG * HD:VC]))
                ve.tensor_tensor(
                    o32[:, b, 2 * half:2 * half + 2, :].rearrange("p t (g h d) -> p (t g) h d", g=G, h=HG),
                    sums[:, :, 0:HG * HD].rearrange("p u (h d) -> p u h d", h=HG),
                    r_.unsqueeze(3).to_broadcast([P, 2 * G, HG, HD]), ALU.mult).then_inc(o_done, 1)

            def halves_low(dst, high, b, high_done, done):
                for half, cols in enumerate(HALVES):
                    low_half(dst[:, b, cols], half_bank[half][:, 0:N // 2], high[:, b, cols], high_done,
                             2 * b + half + 1).then_inc(done, 1)

            def o_low(b):
                halves_low(o_lo, o_hi, b, o_hi_done, o_lo_done)

            def residual(b):
                for half in range(2):
                    tiles = slice(2 * half, 2 * half + 2)
                    dve.wait_ge(attn_ps, 2 * b + half + 1)
                    link(ve.scalar_tensor_tensor(
                        out=x1[:, b, tiles].rearrange("p t d -> p (t d)"), in0=half_bank[half][:, 0:N // 2],
                        scalar=1.0 / (O_SCALE * WO_SCALE), in1=x_sb[:, b, tiles].rearrange("p t d -> p (t d)"),
                        op0=ALU.mult, op1=ALU.add))
                    i_ = stats_of(x1, b, 2 * half, 2 * half + 1)
                moments_of(b, i_)

            def z_low(b):
                halves_low(z_lo, z_hi, b, z_hi_done, z_lo_done)

            def wide(ap):
                return ap.unsqueeze(2).to_broadcast([P, T, E])

            def first_of(b, values_, top, pick):
                link(ve.tensor_reduce(top[:, b, :], values_, AX.X, ALU.max))
                link(ve.tensor_tensor(r_a[:, b], values_, wide(top[:, b, :]), ALU.is_equal))
                link(ve.scalar_tensor_tensor(out=r_b[:, b], in0=r_a[:, b], scalar=-float(E), in1=expert_no[:, :, :],
                                             op0=ALU.mult, op1=ALU.add))
                link(ve.tensor_reduce(least[:, b, :], r_b[:, b], AX.X, ALU.min))
                link(ve.tensor_tensor(pick[:, b], r_b[:, b], wide(least[:, b, :]), ALU.is_equal))

            def choose_first(b):
                dve.wait_ge(logits_ps, b + 1)
                ve.tensor_copy(logits[:, b].rearrange("p t e -> p (t e)"),
                               logits_bank[b][:, 0:T * E]).then_inc(logits_done, 1)
                dve.wait_ge(logits_done, b + 1)
                first_of(b, logits[:, b], top1, pick1)

            def choose_second(b):
                link(ve.scalar_tensor_tensor(out=logits[:, b], in0=pick1[:, b], scalar=MASKED, in1=logits[:, b],
                                             op0=ALU.mult, op1=ALU.add))
                first_of(b, logits[:, b], top2, pick2)
                ve.tensor_tensor(gap[:, b, :], top1[:, b, :], top2[:, b, :], ALU.subtract).then_inc(gap_done, 1)

            def weigh(b):
                dve.wait_ge(th_done, b + 1)
                ve.tensor_scalar(w_1[:, b, :], th[:, b, :], 1.0, half_gate[:, 0:1], ALU.add, ALU.mult)
                link(ve.tensor_scalar(w_2[:, b, :], th[:, b, :], -1.0, half_gate[:, 1:2], ALU.add, ALU.mult))
                ve.tensor_tensor(pick1[:, b], pick1[:, b], wide(w_1[:, b, :]), ALU.mult)
                link(ve.tensor_tensor(pick2[:, b], pick2[:, b], wide(w_2[:, b, :]), ALU.mult))
                link(ve.tensor_tensor(gates[:, b], pick1[:, b], pick2[:, b], ALU.add))
                link(ve.tensor_copy(gates_hl[:, b, :, 0:E], gates[:, b]))
                ve.tensor_tensor(gates_hl[:, b, :, 32:32 + E], gates[:, b], gates_hl[:, b, :, 0:E],
                                 ALU.subtract).then_inc(gates_done, 1)

            def split_hidden(s, k, *halves):
                if not isinstance(s, int) or s >= 2:
                    dve.wait_ge(down_ps, s - 1)
                for j in halves or range(2):
                    chunks = slice(2 * j, 2 * j + 2)
                    if j == 0:
                        dve.wait_ge(gelu_done, C * s + 2)
                        ve.tensor_scalar(h_hi[:, k, chunks, :], h32[k][:, chunks, :], H_SCALE, None,
                                         ALU.mult).then_inc(hi_dve, 1)
                        dve.wait_ge(hi_dve, s + 1)
                    else:
                        dve.wait_ge(hi_act, s + 1)
                    ve.scalar_tensor_tensor(out=h_lo[:, k, chunks, :], in0=h32[k][:, chunks, :], scalar=H_SCALE,
                                            in1=h_hi[:, k, chunks, :], op0=ALU.mult,
                                            op1=ALU.subtract).then_inc(h_split, 1)

            def gate(s, b, e, k, columns=slice(0, N)):
                dve.wait_ge(gate_done, s + 1)
                if not isinstance(s, int) or s >= 2:
                    dve.wait_ge(acc_done, s - 1)
                dve.wait_ge(down_ps, s + 1)
                gates_ = gate_now[:, k, columns] if b else gate_all[:, e, columns]
                ve.scalar_tensor_tensor(out=gated[:, k, columns], in0=down_bank[k][:, columns],
                                        scalar=1.0 / (H_SCALE * W_SCALE * GATE_SCALE), in1=gates_, op0=ALU.mult,
                                        op1=ALU.mult).then_inc(gated_done, 1)

            def accumulate0(e):
                gate(e, 0, e, e % 2)
                dve.wait_ge(acc_begun, 1)
                if e >= 1:
                    dve.wait_ge(acc_done, e)
                dve.wait_ge(gated_done, e + 1)
                ve.tensor_tensor(accT[:, 0, :], accT[:, 0, :], gated[:, e % 2, :], ALU.add).then_inc(acc_done, 1)

            def finish(b, tiles, rows, value):
                dve.wait_ge(out_ps, value)
                ve.tensor_tensor(out_sb[:, b, tiles, :].rearrange("p t d -> p (t d)"), rows,
                                 x1[:, b, tiles, :].rearrange("p t d -> p (t d)"), ALU.add).then_inc(out_done, 1)

            dve.wait_ge(ld_x[0], 16)
            moments_of(0, stats_of(x_sb, 0, *range(T)))
            dve.wait_ge(kT_ps, 1)
            dve.wait_ge(head_mask_done, 1)
            apart(0)
            normalise(xln, x_sb, 0, 1, xln_done)
            apart(1)
            dve.wait_ge(ld_x[1], 16)
            last_stats = stats_of(x_sb, 1, *range(T))
            keys_low(0)
            x_low(0)
            bias_low(0)
            moments_of(1, last_stats)
            maxima(0, 0, 1)
            maxima(0, 2, 3)
            dve.wait_ge(max_consts, 2)
            split_maxima(0)
            dve.wait_ge(ctxT_done, 1)
            ve.tensor_copy(ctxT4[:, :, :, :], ctxT[:, :].rearrange("p (b m) -> p b m", b=B).unsqueeze(2).to_broadcast(
                [P, B, HG, M])).then_inc(ctxT4_done, 1)
            normalise(xln, x_sb, 1, 2, xln_done)
            keys_low(1)
            bias_low(1)
            dve.wait_ge(xT_ps, 2)
            ve.tensor_copy(x_hi[:, 1, :], xT_bank[1][:, :]).then_inc(x_hi_done, 1)
            x_low(1)
            wo_low()
            p_low(0, 0)
            p_low(0, 1)
            maxima(1, 0)
            p_low(0, 2)
            p_low(0, 3)
            maxima(1, 1)
            normalise_heads(0, 0)
            normalise_heads(0, 1)
            maxima(1, 2)
            o_low(0)
            maxima(1, 3)
            split_maxima(1)
            residual(0)
            normalise(zln, x1, 0, B + 1, zln_done)
            for half, cols in enumerate(HALVES):
                dve.wait_ge(zT_ps, half + 1)
                ve.tensor_copy(z_hi[:, 0, cols], half_bank[half][:, 0:N // 2]).then_inc(z_hi_done, 1)
            z_low(0)
            p_low(1, 0)
            dve.wait_ge(gate_consts, 5)
            router_constants()
            p_low(1, 1)
            choose_first(0)
            split_hidden(0, 0)
            choose_second(0)
            split_hidden(1, 1)
            weigh(0)
            split_hidden(2, 0)
            accumulate0(0)
            split_hidden(3, 1)
            accumulate0(1)
            split_hidden(4, 0)
            accumulate0(2)
            normalise_heads(1, 0)
            normalise_heads(1, 1)
            split_hidden(5, 1, 0)
            o_low(1)
            split_hidden(5, 1, 1)
            gate(3, 0, 3, 1)
            residual(1)
            split_hidden(6, 0, 0)
            normalise(zln, x1, 1, B + 2, zln_done)
            split_hidden(6, 0, 1)
            gate(4, 0, 4, 0)
            split_hidden(7, 1, 0)
            z_low(1)
            split_hidden(7, 1, 1)
            gate(5, 0, 5, 1)
            choose_first(1)
            choose_second(1)
            gate(6, 0, 6, 0)
            split_hidden(E, 0, 0)
            weigh(1)
            split_hidden(E, 0, 1)
            gate(7, 0, 7, 1)
            with dve.Fori(0, E // 2 - 1) as pair:
                for k in range(2):
                    s, e = E + 2 * pair + k, 2 * pair + k
                    split_hidden(s + 1, 1 - k)
                    gate(s, 1, e, k)
            split_hidden(S - 1, 1, 0)
            gate(S - 2, 1, E - 2, 0)
            split_hidden(S - 1, 1, 1)
            finish(0, slice(0, T), out0_bank[:, :], 1)
            for half in range(2):
                gate(S - 1, 1, E - 1, 1, HALVES[half])
            for half in range(2):
                finish(1, slice(2 * half, 2 * half + 2), out1_bank[half][:, 0:N // 2], 2 + half)


INS = ["x", "ctx_1024", "g_xattn", "g_ffn", "L0_xattn_Wq", "L0_xattn_bq", "L0_xattn_Wk", "L0_xattn_bk", "L0_xattn_Wv",
       "L0_xattn_bv", "L0_xattn_Wo", "L0_ffn_Wg", "L0_ffn_W1", "L0_ffn_b1", "L0_ffn_W2", "L0_ffn_b2"]


def kernel(**inputs):
    import numpy as np
    import concourse.bacc as bacc
    from concourse.bass_utils import run_bass_kernel_spmd

    nc = bacc.Bacc("TRN2", target_bir_lowering=False, num_devices=1)
    arrays, args = {}, []
    for name in INS:
        a = np.ascontiguousarray(inputs[name])
        arrays[name] = a
        args.append(nc.dram_tensor(name, a.shape, mybir.dt.from_np(a.dtype), kind="ExternalInput").ap())
    out = nc.dram_tensor("out", arrays["x"].shape, F32, kind="ExternalOutput").ap()
    gated_block(nc, *args, out)
    r = run_bass_kernel_spmd(nc, [arrays], core_ids=[0])
    return r.results[0]["out"]
```
